# Optimizing a Trainium2 kernel written in Bass

```python
import numpy as np
import jax
import jax.numpy as jnp

def _softmax(x, axis=-1):
    return jax.nn.softmax(x, axis=axis)

def _gelu(x):
    return jax.nn.gelu(x, approximate=True)

def _silu(x):
    return jax.nn.silu(x)

def _sigmoid(x):
    return jax.nn.sigmoid(x)

def _layernorm(x, axis=-1, eps=1e-05):
    m = jnp.mean(x, axis=axis, keepdims=True)
    v = jnp.var(x, axis=axis, keepdims=True)
    return (x - m) / jnp.sqrt(v + eps)

def _scatter_add(tgt, idx, src, axis=0):
    return tgt.at[idx].add(src)

def _segment_sum(src, seg, n):
    return jax.ops.segment_sum(src, seg, n)
kernel_name = 'mk_adj_preln_d4_adj_r2_a0f541'

def setup_inputs(seed: int=0):
    np.random.seed(seed)
    _w = jnp.asarray

    def _rec_inputs():
        import jax
        import jax.numpy as jnp
        _gk = jax.random.key(seed)
        x = -0.0005207 + 1.001 * jax.random.normal(jax.random.fold_in(_gk, 1), (2048, 256), jnp.float32)
        _a = jax.random.bernoulli(jax.random.fold_in(_gk, 2), 0.00195312, (2048, 2048))
        _a = jnp.logical_or(_a, jnp.swapaxes(_a, -1, -2))
        _a = jnp.logical_or(_a, jnp.eye(2048, dtype=bool))
        _af = _a.astype(jnp.float32)
        adj = _af
        return (x, adj)
    x, adj = _rec_inputs()

    def _L0_gnn_setup():
        import jax, jax.numpy as jnp
        import numpy as np
        N = 2048
        INPUT_DIM = 256
        KEY_DIM = 64
        OUT_DIM = 256
        N_HEADS = 8
        IDENTITY_BIAS = 0.01
        MASK_VAL = 1e+16

        def _xavier(key, shape, gain=np.sqrt(2.0)):
            std = gain * np.sqrt(2.0 / (shape[-2] + shape[-1]))
            return jax.random.normal(key, shape, dtype=jnp.float32) * np.float32(std)
        key = jax.random.key(seed)
        kx, ka, kk, kq, kv, ko = jax.random.split(key, 6)
        node_matrix = jax.random.normal(kx, (N, INPUT_DIM), dtype=jnp.float32)
        adjacency_matrix = jax.random.bernoulli(ka, 0.01, (N, N)).astype(jnp.float32)
        Wks = _xavier(kk, (N_HEADS, INPUT_DIM, KEY_DIM))
        Wqs = _xavier(kq, (N_HEADS, INPUT_DIM, KEY_DIM))
        Wvs = _xavier(kv, (N_HEADS, INPUT_DIM, KEY_DIM))
        Wo = _xavier(ko, (N_HEADS, KEY_DIM, OUT_DIM))
        return {'node_matrix': node_matrix, 'adjacency_matrix': adjacency_matrix, 'Wks': Wks, 'Wqs': Wqs, 'Wvs': Wvs, 'Wo': Wo}
    _L0_gnn_all = _L0_gnn_setup()
    _L0_gnn_in = {k: v for k, v in _L0_gnn_all.items() if k in ('Wks', 'Wqs', 'Wvs', 'Wo')}
    del _L0_gnn_all

    def _L1_gnn_setup():
        import jax, jax.numpy as jnp
        import numpy as np
        N = 4096
        D = 256
        EPS = 1e-12
        key = jax.random.key(seed)
        k1, k2 = jax.random.split(key)
        cur = jax.random.normal(k1, (N, D), dtype=jnp.float32)
        incidence_m = jax.random.normal(k2, (N, N), dtype=jnp.float32)
        return {'cur': cur, 'incidence_m': incidence_m}
    _L1_gnn_all = _L1_gnn_setup()
    _L1_gnn_in = {k: v for k, v in _L1_gnn_all.items() if k in ()}
    del _L1_gnn_all

    def _L2_gnn_setup():
        import jax, jax.numpy as jnp
        import numpy as np
        N = 4096
        D_IN = 256
        D_OUT = 256
        NEG_BIG = -9000000000000000.0
        key = jax.random.key(seed)
        kx, ka, kw, kb, kn, ke = jax.random.split(key, 6)
        x = jax.random.normal(kx, (N, D_IN), dtype=jnp.float32)
        adj = (jax.random.uniform(ka, (N, N)) > 0.9).astype(jnp.float32)
        stdv = 1.0 / np.sqrt(D_OUT)
        weight = jax.random.uniform(kw, (D_IN, D_OUT), minval=-stdv, maxval=stdv, dtype=jnp.float32)
        bias = jax.random.uniform(kb, (D_OUT,), minval=-stdv, maxval=stdv, dtype=jnp.float32)
        node_w = jax.random.uniform(kn, (D_IN, 1), minval=-1.0, maxval=1.0, dtype=jnp.float32)
        stdv_e = 1.0 / np.sqrt(D_IN)
        edge_w = jax.random.uniform(ke, (D_IN, D_IN), minval=-stdv_e, maxval=stdv_e, dtype=jnp.float32)
        return {'x': x, 'adj': adj, 'weight': weight, 'bias': bias, 'node_w': node_w, 'edge_w': edge_w}
    _L2_gnn_all = _L2_gnn_setup()
    _L2_gnn_in = {k: v for k, v in _L2_gnn_all.items() if k in ('weight', 'bias', 'node_w', 'edge_w')}
    del _L2_gnn_all

    def _L3_gnn_setup():
        import jax, jax.numpy as jnp
        import numpy as np
        AVG_DEG = 32
        key = jax.random.key(seed)
        k1, k2, k3 = jax.random.split(key, 3)
        N, D_IN, D_OUT = (4096, 256, 256)
        x = jax.random.normal(k1, (N, D_IN), dtype=jnp.float32)
        u = jax.random.uniform(k2, (N, N), dtype=jnp.float32)
        A = (u < AVG_DEG / (2.0 * N)).astype(jnp.float32)
        A = A + A.T
        A = jnp.clip(A, 0.0, 1.0) * (1.0 - jnp.eye(N, dtype=jnp.float32))
        W = jax.random.normal(k3, (D_OUT, D_IN), dtype=jnp.float32) * (1.0 / np.sqrt(D_IN))
        b = jnp.zeros((D_OUT,), dtype=jnp.float32)
        return {'x': x, 'A': A, 'W': W, 'b': b}
    _L3_gnn_all = _L3_gnn_setup()
    _L3_gnn_in = {k: v for k, v in _L3_gnn_all.items() if k in ('W', 'b')}
    del _L3_gnn_all
    return {'x': x, 'adj': adj, 'L0_gnn_Wks': _L0_gnn_in['Wks'], 'L0_gnn_Wqs': _L0_gnn_in['Wqs'], 'L0_gnn_Wvs': _L0_gnn_in['Wvs'], 'L0_gnn_Wo': _L0_gnn_in['Wo'], 'L2_gnn_weight': _L2_gnn_in['weight'], 'L2_gnn_bias': _L2_gnn_in['bias'], 'L2_gnn_node_w': _L2_gnn_in['node_w'], 'L2_gnn_edge_w': _L2_gnn_in['edge_w'], 'L3_gnn_W': _L3_gnn_in['W'], 'L3_gnn_b': _L3_gnn_in['b']}

def reference(x, adj, L0_gnn_Wks, L0_gnn_Wqs, L0_gnn_Wvs, L0_gnn_Wo, L2_gnn_weight, L2_gnn_bias, L2_gnn_node_w, L2_gnn_edge_w, L3_gnn_W, L3_gnn_b):
    import jax
    import jax.numpy as jnp

    def _L0_gnn_ref(node_matrix, adjacency_matrix, Wks, Wqs, Wvs, Wo):
        import jax, jax.numpy as jnp
        import numpy as np
        N = 2048
        INPUT_DIM = 256
        KEY_DIM = 64
        OUT_DIM = 256
        N_HEADS = 8
        IDENTITY_BIAS = 0.01
        MASK_VAL = 1e+16

        def _xavier(key, shape, gain=np.sqrt(2.0)):
            std = gain * np.sqrt(2.0 / (shape[-2] + shape[-1]))
            return jax.random.normal(key, shape, dtype=jnp.float32) * np.float32(std)
        n = node_matrix.shape[0]
        kd = Wks.shape[-1]
        eye = jnp.eye(n, dtype=node_matrix.dtype)
        adj = jnp.maximum(adjacency_matrix, eye)
        q = jnp.einsum('nd,hdk->hnk', node_matrix, Wqs)
        k = jnp.einsum('nd,hdk->hnk', node_matrix, Wks)
        v = jnp.einsum('nd,hdk->hnk', node_matrix, Wvs)
        scores = jnp.einsum('hqk,hmk->hqm', q, k) * kd ** (-0.5)
        scores = scores + IDENTITY_BIAS * eye - MASK_VAL * (1.0 - adj)
        att = jax.nn.softmax(scores, axis=-1)
        return jnp.einsum('hqm,hmk,hko->qo', att, v, Wo)

    def _L1_gnn_ref(cur, incidence_m):
        import jax, jax.numpy as jnp
        import numpy as np
        N = 4096
        D = 256
        EPS = 1e-12
        mask = incidence_m > 0
        head = jax.lax.stop_gradient(mask.astype(incidence_m.dtype))
        head = head / jnp.maximum(jnp.sqrt(jnp.sum(head * head, axis=-1, keepdims=True)), EPS)
        inc = incidence_m + head
        edge_fea = inc @ cur
        edge_degree = jnp.sum(inc, axis=-1, keepdims=True)
        return edge_fea / edge_degree

    def _L2_gnn_ref(x, adj, weight, bias, node_w, edge_w):
        import jax, jax.numpy as jnp
        import numpy as np
        N = 4096
        D_IN = 256
        D_OUT = 256
        NEG_BIG = -9000000000000000.0
        node_att = jax.nn.softmax(x @ node_w, axis=0)
        h = x @ edge_w
        e = h @ h.T
        e = jnp.where(adj > 0, e, NEG_BIG)
        edge_att = jax.nn.softmax(e, axis=1)
        combined_att = node_att * edge_att
        support = x @ weight
        output = adj * combined_att @ support
        return output + bias

    def _L3_gnn_ref(x, A, W, b):
        import jax, jax.numpy as jnp
        import numpy as np
        AVG_DEG = 32
        N = A.shape[0]
        A_t = A + jnp.eye(N, dtype=A.dtype)
        deg = jnp.sum(A_t, axis=1)
        d_inv_sqrt = jnp.where(deg > 0, jax.lax.rsqrt(deg), 0.0)
        adj_norm = A_t * d_inv_sqrt[:, None] * d_inv_sqrt[None, :]
        h = adj_norm @ x
        out = h @ W.T + b
        return jax.nn.relu(out)
    h = jnp.maximum(_layernorm(x, axis=-1), 0.0)
    x = x + _L0_gnn_ref(h, adj, L0_gnn_Wks, L0_gnn_Wqs, L0_gnn_Wvs, L0_gnn_Wo)
    h = jnp.maximum(_layernorm(x, axis=-1), 0.0)
    x = x + _L1_gnn_ref(h, adj)
    h = jnp.maximum(_layernorm(x, axis=-1), 0.0)
    x = x + _L2_gnn_ref(h, adj, L2_gnn_weight, L2_gnn_bias, L2_gnn_node_w, L2_gnn_edge_w)
    h = jnp.maximum(_layernorm(x, axis=-1), 0.0)
    x = x + _L3_gnn_ref(h, adj, L3_gnn_W, L3_gnn_b)
    return x

_drawn_inputs = setup_inputs


def setup_inputs(seed=0):
    import zlib

    import numpy as np

    out = dict(_drawn_inputs(seed))
    spreads = {'L3_gnn_b': (0.0, 0.393)}
    factors = {'L2_gnn_weight': 8.0, 'L2_gnn_bias': 4.899, 'L2_gnn_node_w': 21.874, 'L2_gnn_edge_w': 8.0}
    for name, (base, spread) in spreads.items():
        noise = np.random.default_rng([zlib.crc32(name.encode()), seed]).standard_normal(out[name].shape)
        drawn = base * np.exp(spread * noise) if base else spread * noise
        out[name] = jnp.asarray(drawn.astype(out[name].dtype))
    for name, factor in factors.items():
        out[name] = (out[name] * factor).astype(out[name].dtype)
    return out
```

```python
from contextlib import ExitStack

import concourse.bass as bass
from concourse import mybir

F32 = mybir.dt.float32
F16 = mybir.dt.float16
BF16 = mybir.dt.bfloat16
ALU = mybir.AluOpType
ACT = mybir.ActivationFunctionType
AX_X = mybir.AxisListType.X
RMAX = bass.bass_isa.ReduceOp.max
RADD = bass.bass_isa.ReduceOp.add

P = 128
N = 2048
D = 256
NT = N // P
DC = D // P
H = 8
KD = 64
PAIRS = H // 2
NCH = NT // 2
CQ = 2 * P
UPC = 4
UPP = NCH * UPC
HALF = N // 2
PROJ = 6
HPP = PROJ + 2 * UPP
GRP = 4
BIG = 2.0 ** 53
IDENTITY_BIAS = 0.01
LN_EPS = 1e-5
NORM_EPS = 1e-12
LOWEST = -3.0e38



def program(nc, x, adj, Wks, Wqs, Wvs, Wo, weight, bias, node_w, edge_w, W3, b3, out, stop=9):
    mask_dram = nc.dram_tensor("mask_rows", (NT, P, N), BF16).ap()
    adjt_dram = nc.dram_tensor("adj_transposed", (NT, P, N), F16).ap()

    def allocators(ctx):
        def sb(name, shape, dt):
            return ctx.enter_context(nc.sbuf_tensor(name, shape, dt))

        def ps(name, shape, dt=F32):
            return ctx.enter_context(nc.psum_tensor(name, shape, dt))

        def sem(name):
            return ctx.enter_context(nc.semaphore(name))
        return sb, ps, sem

    whole = ExitStack()
    sb, _, _ = allocators(whole)
    acc = sb("acc", [P, NT, D], F32)
    ident = sb("ident", [P, P], F32)
    ident16 = sb("ident16", [P, P], F16)
    bias_eye = sb("bias_eye", [P, P], F32)
    mask_eye = sb("mask_eye", [P, P], BF16)
    deg = sb("deg", [P, NT], F32)
    mask_diag = sb("mask_diag", [P, NT, P], BF16)
    stats = sb("stats", [P, NT, 6], F32)
    meanvar = sb("meanvar", [P, NT, 2], F32)
    rstd = sb("rstd", [P, NT], F32)
    nbias = sb("nbias", [P, NT], F32)
    squared = sb("squared", [P, NT], F32)
    root = sb("root", [P, NT], F32)
    tmp = sb("tmp", [P, NT], F32)

    def stand_alone(eng):
        eng.nop(nofuse=True)

    def chained(eng, sem):
        count = [0]

        def link(ins):
            count[0] += 1
            ins.then_inc(sem, 1)
            eng.wait_ge(sem, count[0])
        return link

    def inverse_root(dve, link, squared_ready, root_ready, n):
        dve.sem_inc(squared_ready, 1)
        dve.wait_ge(root_ready, n)
        link(nc.vector.reciprocal(rstd[:], root[:]))
        link(nc.vector.tensor_tensor(tmp[:], rstd[:], rstd[:], ALU.mult))
        link(nc.vector.tensor_tensor(tmp[:], tmp[:], squared[:], ALU.mult))
        link(nc.vector.tensor_scalar(tmp[:], tmp[:], -0.5, 1.5, ALU.mult, ALU.add))
        link(nc.vector.tensor_tensor(rstd[:], rstd[:], tmp[:], ALU.mult))

    def norm_statistics(dve, link, squared_ready, root_ready, n):
        for t in range(NT):
            last = nc.vector.bn_stats(stats[:, t, :], acc[:, t, :])
        link(last)
        for t in range(NT):
            last = nc.vector.bn_aggr(meanvar[:, t, :], stats[:, t, :])
        link(last)
        link(nc.vector.tensor_scalar(squared[:], meanvar[:, :, 1], LN_EPS, None, ALU.add))
        inverse_root(dve, link, squared_ready, root_ready, n)
        link(nc.vector.scalar_tensor_tensor(out=nbias[:], in0=meanvar[:, :, 0], scalar=-1.0, in1=rstd[:],
                                            op0=ALU.mult, op1=ALU.mult))

    def take_root(act, squared_ready, root_ready, n):
        act.wait_ge(squared_ready, n)
        nc.scalar.activation(root[:], squared[:], ACT.Sqrt).then_inc(root_ready, 1)

    def normalise(act, stats_ready, h, h_ready):
        act.wait_ge(stats_ready, 1)
        for t in range(NT):
            nc.scalar.activation(h[:, t, :], acc[:, t, :], ACT.Relu, bias=nbias[:, t:t + 1],
                                 scale=rstd[:, t:t + 1]).then_inc(h_ready, 1)

    def turn_rows(pe, h, h_ready, ps_rows, turned, evacuated):
        for g in range(NT // 2):
            pe.wait_ge(h_ready, 2 * g + 2)
            if g >= 2:
                pe.wait_ge(evacuated, g - 1)
            for dc in range(DC):
                for k in range(2):
                    last = nc.tensor.transpose(ps_rows[:, g % 2, dc, k * P:(k + 1) * P],
                                               h[:, 2 * g + k, dc * P:(dc + 1) * P], ident[:])
            last.then_inc(turned, 1)

    def store_turned(dve, hT, ps_rows, turned, evacuated):
        for g in range(NT // 2):
            dve.wait_ge(turned, g + 1)
            nc.vector.tensor_copy(hT[:, :, g * 2 * P:(g + 1) * 2 * P], ps_rows[:, g % 2])\
                .then_inc(evacuated, 1)

    layer0 = ExitStack()
    sb0, _, _ = allocators(layer0)
    hT = sb0("hT", [P, DC, N], F32)

    with ExitStack() as ctx:
        sb, ps, sem = allocators(ctx)
        h = sb("h_in", [P, NT, D], F32)
        adj_in = sb("adj_in", [P, 2, N], F32)
        adj16 = sb("adj16", [P, 2, N], F16)
        mask = sb("mask", [P, 2, N], BF16)
        adjt = sb("adjt_stage", [P, 2, N], F16)
        ps_rows = ps("ps_rows", [P, 2, DC, 2 * P])
        ps_adjt = ps("ps_adjt", [P, 2, N], F16)

        x_in = sem("x_in")
        adj_loaded = [sem(f"adj_loaded{k}") for k in range(2)]
        filled, consts = sem("consts_filled"), sem("consts_ready")
        steps, squared_ready, root_ready, stats_ready = (sem(f"{s}_in") for s in ("steps", "sq", "root", "stats"))
        h_ready, turned, evacuated = (sem(f"{s}_in") for s in ("h_ready", "turned", "evacuated"))
        adj_copied = sem("adj_copied")
        mask_written = sem("mask_written")
        masked = sem("masked_in")
        adj_turned = sem("adj_turned")
        adjt_staged = sem("adjt_staged")
        mask_out = [sem(f"mask_out{k}") for k in range(2)]
        adjt_out = [sem(f"adjt_out{k}") for k in range(2)]

        with nc.Block() as block:
            @block.sync
            def _(sp):
                sp.dma_start(acc[:], x.rearrange("(t p) d -> p t d", p=P)).then_inc(x_in, 16)
                with sp.Fori(0, NT // 2) as i2:
                    for k in range(2):
                        sp.wait_ge(adj_copied, 2 * i2 + k + 1)
                        sp.wait_ge(masked, 2 * i2 + k + 1)
                        sp.dma_start(adj_in[:, k, :], adj[bass.ds((2 * i2 + k) * P, P), :])\
                            .then_inc(adj_loaded[k], 16)

            @block.gpsimd
            def _(pool):
                nc.gpsimd.memset(ident[:], 0.0).then_inc(filled, 1)
                nc.gpsimd.memset(ident16[:], 0.0).then_inc(filled, 1)
                nc.gpsimd.memset(bias_eye[:], 0.0).then_inc(filled, 1)
                nc.gpsimd.memset(mask_eye[:], -BIG).then_inc(filled, 1)
                pool.wait_ge(filled, 4)
                for m, v in ((ident, 1.0), (ident16, 1.0), (bias_eye, IDENTITY_BIAS), (mask_eye, 0.0)):
                    nc.gpsimd.affine_select(out=m[:], in_=m[:], compare_op=ALU.not_equal, fill=v, base=0,
                                            pattern=[[-1, P]], channel_multiplier=1).then_inc(consts, 1)
                with pool.Fori(0, NT // 2) as i2:
                    for k in range(2):
                        pool.wait_ge(masked, 2 * i2 + k + 3)
                        stand_alone(pool)
                        pool.dma_start(mask_dram[2 * i2 + k], mask[:, k, :]).then_inc(mask_out[k], 16)
                        pool.wait_ge(adjt_staged, 2 * i2 + k + 3)
                        stand_alone(pool)
                        pool.dma_start(adjt_dram[2 * i2 + k], adjt[:, k, :]).then_inc(adjt_out[k], 16)
                for k in range(2):
                    pool.wait_ge(mask_out[k], 16 * NT // 2)
                    pool.wait_ge(adjt_out[k], 16 * NT // 2)

            @block.scalar
            def _(act):
                act.sem_inc(adj_copied, 2)
                take_root(act, squared_ready, root_ready, 1)
                normalise(act, stats_ready, h, h_ready)
                with act.Fori(0, NT // 2) as i2:
                    for k in range(2):
                        act.wait_ge(adj_loaded[k], 16 * i2 + 16)
                        act.wait_ge(adj_turned, 2 * i2 + k + 1)
                        nc.scalar.activation(adj16[:, k, :], adj_in[:, k, :], ACT.Copy,
                                             accum_out=deg[:, bass.ds(2 * i2 + k, 1)]).then_inc(adj_copied, 1)

            @block.tensor
            def _(pe):
                pe.sem_inc(adj_turned, 2)
                pe.wait_ge(consts, 4)
                turn_rows(pe, h, h_ready, ps_rows, turned, evacuated)
                with pe.Fori(0, NT // 2) as i2:
                    for k in range(2):
                        pe.wait_ge(adj_copied, 2 * i2 + k + 3)
                        pe.wait_ge(adjt_staged, 2 * i2 + k + 1)
                        for j in range(NT):
                            last = nc.tensor.transpose(ps_adjt[:, k, j * P:(j + 1) * P],
                                                       adj16[:, k, j * P:(j + 1) * P], ident16[:])
                        last.then_inc(adj_turned, 1)

            @block.vector
            def _(dve):
                dve.sem_inc(masked, 2)
                dve.sem_inc(adjt_staged, 2)
                link = chained(dve, steps)
                dve.wait_ge(x_in, 16)
                norm_statistics(dve, link, squared_ready, root_ready, 1)
                dve.sem_inc(stats_ready, 1)
                store_turned(dve, hT, ps_rows, turned, evacuated)
                dve.wait_ge(consts, 4)

                def masks_of(i2, first):
                    for k in range(2):
                        t = 2 * i2 + k
                        dve.wait_ge(adj_loaded[k], 16 * i2 + 16)
                        if not first:
                            dve.wait_ge(mask_out[k], 16 * i2)
                        nc.vector.tensor_scalar(mask[:, k, :], adj_in[:, k, :], -1.0, BIG, ALU.add, ALU.mult)\
                            .then_inc(mask_written, 1)
                        dve.wait_ge(mask_written, 2 * t + 1)
                        diag = mask[:, k, bass.ds(t * P, P)]
                        nc.vector.tensor_copy(mask_diag[:, bass.ds(t, 1), :], diag).then_inc(mask_written, 1)
                        dve.wait_ge(mask_written, 2 * t + 2)
                        nc.vector.tensor_tensor(diag, diag, mask_eye[:], ALU.max).then_inc(masked, 1)
                        dve.wait_ge(adj_turned, t + 3)
                        if not first:
                            dve.wait_ge(adjt_out[k], 16 * i2)
                        nc.vector.tensor_copy(adjt[:, k, :], ps_adjt[:, k, :]).then_inc(adjt_staged, 1)

                masks_of(0, True)
                with dve.Fori(1, NT // 2) as i2:
                    masks_of(i2, False)

    if stop >= 1:
        with ExitStack() as ctx:
            sb, ps, sem = allocators(ctx)
            w_pair = sb("w_pair", [P, 3, DC, 2 * KD], F32)
            wo_sb = sb("wo_sb", [P, PAIRS, D], F32)
            q_parts = sb("q_parts", [P, 2, N], F16)
            k_parts = sb("k_parts", [P, 2, 2, N], F16)
            v_sb = sb("v_sb", [P, NT, 2 * KD], F32)
            mask = sb("mask0", [P, 2, N], BF16)
            probs = sb("probs", [P, UPC, N], F32)
            probs_t = sb("probs_t", [P, 2, 2, NT, CQ], F32)
            row_max = sb("row_max", [P, UPC, 2], F32)
            neg_max = sb("neg_max", [P, UPC], F32)
            den = sb("den", [P, 2, UPC], F32)
            rden = sb("rden", [P, UPC], F32)
            rden_rows = sb("rden_rows", [P, UPC, KD], F32)
            rden_t = sb("rden_t", [P, CQ], F32)
            o_normed = sb("o_normed", [P, CQ], F32)
            ps_s = ps("ps_s", [P, 2, HALF])
            ps_ta = ps("ps_ta", [P, GRP * P])
            ps_td = ps("ps_td", [P, GRP * P])
            ps_o = ps("ps_o", [P, 512])
            ps_x = ps("ps_x", [P, 512])

            w_in, wo_in = sem("w_in"), sem("wo_in")
            mask_in = [sem(f"mask_in{k}") for k in range(2)]
            half_full = sem("half_full")
            half_free = sem("half_free")
            hi_ready = sem("hi_ready")
            masked = sem("masked")
            exped = sem("exped")
            ta_full, ta_free = sem("ta_full"), sem("ta_free")
            td_full, td_free = sem("td_full"), sem("td_free")
            pv_done = sem("pv_done")
            rden_ready = sem("rden_ready")
            rden_turned = sem("rden_turned")
            rden_t_ready = sem("rden_t_ready")
            o_ready = sem("o_ready")
            out_ready = sem("out_ready")
            added = sem("added")
            steps = sem("steps0")

            def each_chunk(eng, pair, body):
                body(0, 0, True, False)
                with eng.Fori(0, (NCH - 2) // 2) as i:
                    body(2 * i + 1, 1, False, False)
                    body(2 * i + 2, 0, False, False)
                body(NCH - 1, 1, False, True)

            with nc.Block() as block:
                @block.sync
                def _(sp):
                    with sp.Fori(0, PAIRS) as pair:
                        with sp.Fori(0, NCH) as c:
                            for k in range(2):
                                sp.wait_ge(masked, UPP * pair + UPC * c + 2 * k + 2)
                                sp.dma_start(mask[:, k, :], mask_dram[2 * c + k]).then_inc(mask_in[k], 16)

                @block.gpsimd
                def _(pool):
                    pool.dma_start(wo_sb[:], Wo.rearrange("(g a) k o -> (a k) g o", a=2)).then_inc(wo_in, 16)

                    def load_pair(pair):
                        for n, w in enumerate((Wqs, Wks, Wvs)):
                            for a in range(2):
                                pool.dma_start(
                                    w_pair[:, n, :, a * KD:(a + 1) * KD],
                                    w[bass.ds(2 * pair + a, 1)].rearrange("h (c p) k -> p (h c) k", p=P))\
                                    .then_inc(w_in, 16)

                    load_pair(0)
                    with pool.Fori(1, PAIRS) as pair:
                        pool.wait_ge(half_full, HPP * (pair - 1) + PROJ)
                        stand_alone(pool)
                        load_pair(pair)

                @block.tensor
                def _(pe):
                    pe.sem_inc(td_full, 8)
                    pe.sem_inc(pv_done, 2)
                    pe.wait_ge(wo_in, 16)
                    with pe.Fori(0, PAIRS) as pair:
                        def free_half(n):
                            pe.wait_ge(half_free, HPP * pair + n + 1)

                        def scores(u, q_tile, head, half):
                            free_half(PROJ + 2 * u + half)
                            for n in range(2):
                                cols = slice(half * HALF + n * 512, half * HALF + (n + 1) * 512)
                                for part in range(2):
                                    last = nc.tensor.matmul(ps_s[:, half, n * 512:(n + 1) * 512],
                                                            q_parts[:, head, bass.ds(q_tile * P, P)],
                                                            k_parts[:, head, part, cols],
                                                            start=(part == 0), stop=(part == 1))
                            last.then_inc(half_full, 1)

                        def turn(g, w, grp):
                            bank, free, full = ((ps_ta, ta_free, ta_full), (ps_td, td_free, td_full))[grp % 2]
                            pe.wait_ge(free, 2 * g + grp // 2 + 1)
                            for k in range(GRP):
                                j = GRP * grp + k
                                last = nc.tensor.transpose(bank[:, k * P:(k + 1) * P],
                                                           probs[:, w, j * P:(j + 1) * P], ident[:])
                            last.then_inc(full, 1)

                        def attend(chunk, parity, js):
                            if js[0] == 0:
                                pe.wait_ge(ta_free, 2 * UPC * (chunk + 1) + 1)
                                pe.wait_ge(td_free, 2 * UPC * (chunk + 1) + 1)
                                pe.wait_ge(o_ready, chunk + 1)
                            for j in js:
                                for a in range(2):
                                    last = nc.tensor.matmul(ps_o[a * KD:(a + 1) * KD, 0:CQ],
                                                            v_sb[:, j, a * KD:(a + 1) * KD],
                                                            probs_t[:, parity, a, j, :],
                                                            start=(j == 0), stop=(j == NT - 1),
                                                            skip_group_check=True)
                            if js[-1] == NT - 1:
                                last.then_inc(pv_done, 1)

                        def turn_rden(chunk):
                            pe.wait_ge(rden_ready, chunk + 1)
                            pe.wait_ge(added, chunk + 1)
                            for k in range(2):
                                last = nc.tensor.transpose(ps_x[:, k * P:(k + 1) * P],
                                                           rden_rows[:, 2 * k:2 * k + 2, :]
                                                           .rearrange("p a k -> p (a k)"), ident[:])
                            last.then_inc(rden_turned, 1)

                        def project_out(chunk, pair):
                            pe.wait_ge(o_ready, chunk + 2)
                            for k in range(2):
                                last = nc.tensor.matmul(ps_x[:, k * D:(k + 1) * D], o_normed[:, k * P:(k + 1) * P],
                                                        wo_sb[:, bass.ds(pair, 1), :]
                                                        .rearrange("p g o -> p (g o)"), start=True, stop=True)
                            last.then_inc(out_ready, 1)

                        pe.wait_ge(w_in, 6 * 16 * (pair + 1))
                        for n in range(2):
                            for half in range(2):
                                free_half(2 * n + half)
                                for c in range(2):
                                    for dc in range(DC):
                                        first = half * HALF + c * 512
                                        last = nc.tensor.matmul(ps_s[:, half, c * 512:(c + 1) * 512],
                                                                w_pair[:, n, dc, :], hT[:, dc, first:first + 512],
                                                                start=(dc == 0), stop=(dc == DC - 1))
                                last.then_inc(half_full, 1)
                        for half in range(2):
                            free_half(4 + half)
                            for t in range(NT // 2):
                                for dc in range(DC):
                                    first = (half * NT // 2 + t) * P
                                    last = nc.tensor.matmul(ps_s[:, half, t * P:(t + 1) * P],
                                                            hT[:, dc, first:first + P], w_pair[:, 2, dc, :],
                                                            start=(dc == 0), stop=(dc == DC - 1))
                            last.then_inc(half_full, 1)

                        for half in range(2):
                            scores(0, 0, 0, half)

                        def chunk_body(c, parity, first, last_one):
                            chunk = NCH * pair + c
                            for w in range(UPC):
                                g = UPC * chunk + w
                                more = not (last_one and w == UPC - 1)
                                w1 = (w + 1) % UPC
                                q_tile = 2 * c + (w + 1) // 2
                                if more:
                                    scores(UPC * c + w + 1, q_tile, w1 % 2, 0)
                                pe.wait_ge(exped, g + 1)
                                turn(g, w, 0)
                                turn(g, w, 1)
                                if w == 3 and not first:
                                    project_out(chunk - 1, pair)
                                if more:
                                    scores(UPC * c + w + 1, q_tile, w1 % 2, 1)
                                turn(g, w, 2)
                                turn(g, w, 3)
                                if not first:
                                    if w < 3:
                                        attend(chunk - 1, 1 - parity, (range(0, 6), range(6, 11), range(11, 16))[w])
                                    if w == 1:
                                        turn_rden(chunk - 1)

                        each_chunk(pe, pair, chunk_body)
                        final = NCH * pair + NCH - 1
                        turn_rden(final)
                        attend(final, 1, range(NT))
                        project_out(final, pair)

                @block.scalar
                def _(act):
                    act.sem_inc(ta_free, 1)
                    with act.Fori(0, PAIRS) as pair:
                        for half in range(2):
                            act.wait_ge(half_full, HPP * pair + half + 1)
                            cols = slice(half * HALF, (half + 1) * HALF)
                            for a in range(2):
                                last = nc.scalar.activation(q_parts[0:KD, a, cols], ps_s[a * KD:(a + 1) * KD, half, :],
                                                            ACT.Copy, scale=KD ** -0.5)
                            last.then_inc(hi_ready, 1)
                        for half in range(2):
                            act.wait_ge(half_full, HPP * pair + 2 + half + 1)
                            cols = slice(half * HALF, (half + 1) * HALF)
                            for a in range(2):
                                for b in range(2):
                                    last = nc.scalar.activation(k_parts[b * KD:(b + 1) * KD, a, 0, cols],
                                                                ps_s[a * KD:(a + 1) * KD, half, :], ACT.Copy)
                            last.then_inc(hi_ready, 1)

                        def exponentials(g, w, parity):
                            act.wait_ge(masked, g + UPC + 1)
                            nc.scalar.activation(probs[:, w, :], probs[:, w, :], ACT.Exp, bias=neg_max[:, w:w + 1],
                                                 accum_out=den[:, parity, w:w + 1]).then_inc(exped, 1)

                        def copy_rden(chunk):
                            act.wait_ge(rden_turned, chunk + 1)
                            nc.scalar.activation(rden_t[:], ps_x[:, 0:CQ], ACT.Copy).then_inc(rden_t_ready, 1)

                        exponentials(UPP * pair, 0, 0)

                        def chunk_body(c, parity, first, last_one):
                            chunk = NCH * pair + c
                            act.wait_ge(pv_done, chunk + 1)
                            for w in range(UPC):
                                g = UPC * chunk + w
                                if w == 2 and not first:
                                    copy_rden(chunk - 1)
                                for k in range(2):
                                    act.wait_ge(ta_full, 2 * g + k + 1)
                                    first_j = 2 * GRP * k
                                    nc.scalar.activation(
                                        probs_t[:, parity, w % 2, first_j:first_j + GRP, w // 2 * P:(w // 2 + 1) * P],
                                        ps_ta[:].rearrange("p (j q) -> p j q", q=P), ACT.Copy).then_inc(ta_free, 1)
                                if not (last_one and w == UPC - 1):
                                    exponentials(g + 1, (w + 1) % UPC, parity if w < UPC - 1 else 1 - parity)

                        each_chunk(act, pair, chunk_body)
                        copy_rden(NCH * pair + NCH - 1)

                @block.vector
                def _(dve):
                    dve.sem_inc(half_free, 2)
                    dve.sem_inc(masked, 4)
                    dve.sem_inc(td_free, 1)
                    dve.sem_inc(o_ready, 1)
                    dve.sem_inc(added, 1)
                    with dve.Fori(0, PAIRS) as pair:
                        for half in range(2):
                            dve.wait_ge(hi_ready, 4 * pair + half + 1)
                            cols = slice(half * HALF, (half + 1) * HALF)
                            for a in range(2):
                                last = nc.vector.scalar_tensor_tensor(
                                    out=q_parts[KD:P, a, cols], in0=ps_s[a * KD:(a + 1) * KD, half, :],
                                    scalar=KD ** -0.5, in1=q_parts[0:KD, a, cols], op0=ALU.mult, op1=ALU.subtract)
                            last.then_inc(half_free, 1)
                        for half in range(2):
                            dve.wait_ge(hi_ready, 4 * pair + 2 + half + 1)
                            cols = slice(half * HALF, (half + 1) * HALF)
                            for a in range(2):
                                for b in range(2):
                                    rows = slice(b * KD, (b + 1) * KD)
                                    last = nc.vector.tensor_tensor(
                                        k_parts[rows, a, 1, cols], ps_s[a * KD:(a + 1) * KD, half, :],
                                        k_parts[rows, a, 0, cols], ALU.subtract)
                            last.then_inc(half_free, 1)
                        for half in range(2):
                            dve.wait_ge(half_full, HPP * pair + 4 + half + 1)
                            nc.vector.tensor_copy(v_sb[:, half * NT // 2:(half + 1) * NT // 2, :],
                                                  ps_s[:, half, :].rearrange("p (t k) -> p t k", k=2 * KD))\
                                .then_inc(half_free, 1)

                        def mask_half(g, u, w, half):
                            dve.wait_ge(half_full, HPP * pair + PROJ + 2 * u + half + 1)
                            if half == 0:
                                dve.wait_ge(td_full, 2 * g + 2)
                            stand_alone(dve)
                            nc.vector.tensor_tensor_reduce(
                                probs[:, w, half * HALF:(half + 1) * HALF], ps_s[:, half, :],
                                mask[:, w // 2, half * HALF:(half + 1) * HALF], 1.0, LOWEST, ALU.add, ALU.max,
                                row_max[:, w, half:half + 1]).then_inc(half_free, 1)

                        def finish_mask(g, u, w, q_tile):
                            dve.wait_ge(half_free, HPP * pair + PROJ + 2 * u + 4)
                            nc.vector.tensor_reduce(neg_max[:, w:w + 1], row_max[:, w, :], AX_X, ALU.max, negate=True)
                            diag = probs[:, w, bass.ds(q_tile * P, P)]
                            nc.vector.tensor_tensor(diag, diag, bias_eye[:], ALU.add).then_inc(masked, 1)

                        def copy_group(g, w, parity, k):
                            dve.wait_ge(td_full, 2 * g + k + 9)
                            first_j = GRP + 2 * GRP * k
                            nc.vector.tensor_copy(
                                probs_t[:, parity, w % 2, first_j:first_j + GRP, w // 2 * P:(w // 2 + 1) * P],
                                ps_td[:].rearrange("p (j q) -> p j q", q=P)).then_inc(td_free, 1)

                        def spread_rden(chunk, parity):
                            nc.vector.reciprocal(rden[:], den[:, parity, :]).then_inc(steps, 1)
                            dve.wait_ge(steps, chunk + 1)
                            nc.vector.tensor_copy(rden_rows[:], rden[:].unsqueeze(2).to_broadcast([P, UPC, KD]))\
                                .then_inc(rden_ready, 1)

                        def normalise_out(chunk):
                            dve.wait_ge(pv_done, chunk + 3)
                            dve.wait_ge(rden_t_ready, chunk + 1)
                            nc.vector.tensor_tensor(o_normed[:], ps_o[:, 0:CQ], rden_t[:], ALU.mult).then_inc(o_ready, 1)

                        def add_out(chunk, c):
                            dve.wait_ge(out_ready, chunk + 1)
                            rows = acc[:, bass.ds(2 * c, 2), :]
                            nc.vector.tensor_tensor(rows, ps_x[:].rearrange("p (t d) -> p t d", d=D), rows, ALU.add)\
                                .then_inc(added, 1)

                        dve.wait_ge(mask_in[0], 16 * NCH * pair + 16)
                        for half in range(2):
                            mask_half(UPP * pair, 0, 0, half)
                        finish_mask(UPP * pair, 0, 0, 0)

                        def chunk_body(c, parity, first, last_one):
                            chunk = NCH * pair + c
                            dve.wait_ge(pv_done, chunk + 1)
                            for w in range(UPC):
                                g = UPC * chunk + w
                                u1, w1 = UPC * c + w + 1, (w + 1) % UPC
                                more = not (last_one and w == UPC - 1)
                                if w == 0 and not first:
                                    spread_rden(chunk - 1, 1 - parity)
                                if w == 3 and not first:
                                    normalise_out(chunk - 1)
                                if more:
                                    if w1 % 2 == 0:
                                        dve.wait_ge(mask_in[w1 // 2], 16 * (chunk + (w + 1) // UPC) + 16)
                                    mask_half(g + 1, u1, w1, 0)
                                copy_group(g, w, parity, 0)
                                if more:
                                    mask_half(g + 1, u1, w1, 1)
                                    finish_mask(g + 1, u1, w1, 2 * c + (w + 1) // 2)
                                copy_group(g, w, parity, 1)
                                if w == 3 and not first:
                                    add_out(chunk - 1, c - 1)

                        each_chunk(dve, pair, chunk_body)
                        final = NCH * pair + NCH - 1
                        dve.wait_ge(exped, UPP * (pair + 1))
                        spread_rden(final, 1)
                        normalise_out(final)
                        add_out(final, NCH - 1)
    layer0.close()

    late = ExitStack()
    sb, _, _ = allocators(late)
    adjt = sb("adjt", [P, NT, NT, P], F16)
    h = sb("h", [P, NT, D], F32)
    row_scale = sb("row_scale", [P, NT], F32)

    def split_rows(dve, h_parts, parts_ready):
        for t in range(0, NT, 2):
            hi, lo = (h_parts[:, t:t + 2, k, :] for k in range(2))
            nc.vector.tensor_copy(hi, h[:, t:t + 2, :]).then_inc(parts_ready, 1)
            dve.wait_ge(parts_ready, t + 1)
            nc.vector.tensor_tensor(lo, h[:, t:t + 2, :], hi, ALU.subtract).then_inc(parts_ready, 1)

    def gather(t, bank, h_parts, ps_g, js):
        for j in js:
            last = nc.tensor.matmul(ps_g[:, bank, :], adjt[:, bass.ds(t, 1), j, :].rearrange("p a q -> p (a q)"),
                                    h_parts[:, j].rearrange("p a d -> p (a d)"),
                                    start=(j == 0), stop=(j == NT - 1))
        return last

    if stop >= 2:
        with ExitStack() as ctx:
            sb, ps, sem = allocators(ctx)
            inv_norm = sb("inv_norm", [P, NT], F32)
            inc_scale = sb("inc_scale", [P, NT], F32)
            h_parts = sb("h_parts1", [P, NT, 2, D], F16)
            ps_g = ps("ps_g1", [P, 2, 2 * D])
            adjt_in = sem("adjt_in")
            steps, squared_ready, root_ready, stats_ready = (sem(f"{s}_1") for s in ("steps", "sq", "root", "stats"))
            h_ready, parts_ready = sem("h_ready1"), sem("parts_ready1")
            gathered = sem("gathered1")
            half_added = sem("half_added1")
            taken = sem("taken1")

            with nc.Block() as block:
                @block.sync
                def _(sp):
                    with sp.Fori(0, NT) as t:
                        sp.dma_start(adjt[:, bass.ds(t, 1)].rearrange("p t j q -> p (t j q)"), adjt_dram[t])\
                            .then_inc(adjt_in, 16)
                    sp.wait_ge(adjt_in, 16 * NT)

                @block.scalar
                def _(act):
                    take_root(act, squared_ready, root_ready, 1)
                    act.wait_ge(squared_ready, 2)
                    nc.scalar.activation(root[:], deg[:], ACT.Sqrt).then_inc(root_ready, 1)
                    normalise(act, stats_ready, h, h_ready)

                @block.tensor
                def _(pe):
                    pe.wait_ge(adjt_in, 16 * NT)
                    pe.wait_ge(parts_ready, NT)
                    with pe.Fori(0, NT // 2) as i2:
                        for k in range(2):
                            pe.wait_ge(taken, 2 * i2 + k + 1)
                            gather(2 * i2 + k, k, h_parts, ps_g, range(NT)).then_inc(gathered, 1)

                @block.vector
                def _(dve):
                    dve.sem_inc(taken, 2)
                    link = chained(dve, steps)
                    norm_statistics(dve, link, squared_ready, root_ready, 1)
                    dve.sem_inc(stats_ready, 1)
                    dve.sem_inc(squared_ready, 1)
                    dve.wait_ge(root_ready, 2)
                    link(nc.vector.tensor_scalar(tmp[:], root[:], NORM_EPS, None, ALU.max))
                    link(nc.vector.reciprocal(inv_norm[:], tmp[:]))
                    link(nc.vector.tensor_scalar(inc_scale[:], inv_norm[:], 1.0, None, ALU.add))
                    link(nc.vector.tensor_tensor(tmp[:], inc_scale[:], deg[:], ALU.mult))
                    link(nc.vector.reciprocal(row_scale[:], tmp[:]))
                    link(nc.vector.tensor_tensor(row_scale[:], row_scale[:], inc_scale[:], ALU.mult))
                    dve.wait_ge(h_ready, NT)
                    split_rows(dve, h_parts, parts_ready)
                    with dve.Fori(0, NT // 2) as i2:
                        for k in range(2):
                            t = 2 * i2 + k
                            rows = acc[:, bass.ds(t, 1), :].rearrange("p t d -> p (t d)")
                            scale = row_scale[:, bass.ds(t, 1)]
                            dve.wait_ge(gathered, t + 1)
                            nc.vector.scalar_tensor_tensor(out=rows, in0=ps_g[:, k, 0:D], scalar=scale,
                                                           in1=rows, op0=ALU.mult, op1=ALU.add)\
                                .then_inc(half_added, 1)
                            dve.wait_ge(half_added, t + 1)
                            nc.vector.scalar_tensor_tensor(out=rows, in0=ps_g[:, k, D:2 * D], scalar=scale,
                                                           in1=rows, op0=ALU.mult, op1=ALU.add).then_inc(taken, 1)

    if stop >= 3:
        with ExitStack() as ctx:
            sb, ps, sem = allocators(ctx)
            hT = sb("hT2", [P, DC, N], F32)
            eT = sb("eT", [P, DC, N], F32)
            support = sb("support", [P, NT, D], F32)
            weight_sb = sb("weight_sb", [P, DC, D], F32)
            edge_sb = sb("edge_sb", [P, DC, D], F32)
            bias_rows = sb("bias_rows", [P, D], F32)
            node_rows = sb("node_rows", [P, D], F32)
            logits = sb("logits", [P, NT], F32)
            node_max = sb("node_max", [P, 3], F32)
            node_sum = sb("node_sum", [P, 3], F32)
            node_att = sb("node_att", [P, NT], F32)
            has_edge = sb("has_edge", [P, NT], F32)
            e_tile = sb("e_tile", [P, 2, DC, P], F32)
            mask = sb("mask2", [P, 2, N], BF16)
            probs = sb("probs2", [P, 2, N], F32)
            probs_t = sb("probs_t2", [P, 2, NT, P], F32)
            products = probs[:].rearrange("p k (t d) -> p (k t) d", d=D)
            row_max = sb("row_max2", [P, 2, 2], F32)
            neg_max = sb("neg_max2", [P, 2], F32)
            den = sb("den2", [P, 2], F32)
            rden = sb("rden2", [P, 2], F32)
            ps_s = ps("ps_s2", [P, 2, HALF])
            ps_ta = ps("ps_ta2", [P, GRP * P])
            ps_td = ps("ps_td2", [P, GRP * P])
            ps_o = ps("ps_o2", [P, 2, 512])
            ps_rows = ps_o[:].rearrange("p b (c q) -> p b c q", c=DC)

            w_in = sem("w_in2")
            steps, squared_ready, root_ready, stats_ready = (sem(f"{s}_2") for s in ("steps", "sq", "root", "stats"))
            h_ready, turned, evacuated = (sem(f"{s}_2") for s in ("h_ready", "turned", "evacuated"))
            proj_full = sem("proj_full2")
            proj_free = sem("proj_free2")
            max_ready, all_max, neg_ready = sem("max_ready"), sem("all_max"), sem("neg_ready")
            node_exp, all_sum = sem("node_exp"), sem("all_sum")
            mask_in = [sem(f"mask_in2{k}") for k in range(2)]
            mask_patched = sem("mask_patched")
            tile_ready = sem("tile_ready2")
            half_full = sem("half_full2")
            half_free = sem("half_free2")
            masked = sem("masked2")
            exped = sem("exped2")
            ta_full, ta_free = sem("ta_full2"), sem("ta_free2")
            td_full, td_free = sem("td_full2"), sem("td_free2")
            pv_done = sem("pv_done2")
            scale_steps = sem("scale_steps2")
            added = sem("added2")
            NPROJ = 4 + 4

            def each_tile(eng, body):
                with eng.Fori(0, NT // 2 - 1) as i:
                    body(2 * i, 0, True)
                    body(2 * i + 1, 1, True)
                body(NT - 2, 0, True)
                body(NT - 1, 1, False)

            with nc.Block() as block:
                @block.sync
                def _(sp):
                    sp.dma_start(edge_sb[:], edge_w.rearrange("(c p) o -> p c o", p=P)).then_inc(w_in, 16)
                    sp.dma_start(weight_sb[:], weight.rearrange("(c p) o -> p c o", p=P)).then_inc(w_in, 16)
                    sp.dma_start(node_rows[:], node_w.rearrange("d a -> (d a)").partition_broadcast(P))\
                        .then_inc(w_in, 16)
                    sp.dma_start(bias_rows[:], bias.partition_broadcast(P)).then_inc(w_in, 16)
                    with sp.Fori(0, NT // 2) as i2:
                        for k in range(2):
                            sp.wait_ge(masked, 2 * i2 + k + 1)
                            sp.dma_start(mask[:, k, :], mask_dram[2 * i2 + k]).then_inc(mask_in[k], 16)

                @block.gpsimd
                def _(pool):
                    pool.wait_ge(max_ready, 1)
                    nc.gpsimd.partition_all_reduce(node_max[:, 1:2], node_max[:, 0:1], P, RMAX).then_inc(all_max, 1)
                    pool.wait_ge(node_exp, 1)
                    nc.gpsimd.partition_all_reduce(node_sum[:, 1:2], node_sum[:, 0:1], P, RADD).then_inc(all_sum, 1)
                    pool.wait_ge(proj_free, 2 + 4)
                    with pool.Fori(0, NT // 2) as i2:
                        for k in range(2):
                            t = 2 * i2 + k
                            pool.wait_ge(half_full, 2 * t + 2)
                            nc.gpsimd.tensor_copy(e_tile[:, k], eT[:, :, bass.ds(t * P, P)])\
                                .then_inc(tile_ready, 1)

                @block.tensor
                def _(pe):
                    pe.sem_inc(half_full, 4)
                    pe.sem_inc(td_full, 4)
                    pe.sem_inc(pv_done, 2)
                    turn_rows(pe, h, h_ready, ps_rows, turned, evacuated)
                    pe.wait_ge(evacuated, NT // 2)
                    pe.wait_ge(w_in, 4 * 16)
                    for n in range(4):
                        oc, half = n // 2, n % 2
                        pe.wait_ge(proj_free, n + 1)
                        for c in range(2):
                            first = half * HALF + c * 512
                            for dc in range(DC):
                                last = nc.tensor.matmul(ps_s[:, half, c * 512:(c + 1) * 512],
                                                        edge_sb[:, dc, oc * P:(oc + 1) * P],
                                                        hT[:, dc, first:first + 512],
                                                        start=(dc == 0), stop=(dc == DC - 1))
                        last.then_inc(proj_full, 1)
                    for n in range(4):
                        pe.wait_ge(proj_free, 4 + n + 1)
                        for t in range(4):
                            first = (4 * n + t) * P
                            for dc in range(DC):
                                last = nc.tensor.matmul(ps_s[:, n % 2, t * D:(t + 1) * D],
                                                        hT[:, dc, first:first + P], weight_sb[:, dc, :],
                                                        start=(dc == 0), stop=(dc == DC - 1))
                        last.then_inc(proj_full, 1)
                    pe.wait_ge(proj_free, NPROJ + 2)

                    def scores(t, k, half):
                        pe.wait_ge(tile_ready, t + 1)
                        pe.wait_ge(half_free, 2 * t + half + 1)
                        for c in range(2):
                            first = half * HALF + c * 512
                            for dc in range(DC):
                                last = nc.tensor.matmul(ps_s[:, half, c * 512:(c + 1) * 512], e_tile[:, k, dc, :],
                                                        eT[:, dc, first:first + 512],
                                                        start=(dc == 0), stop=(dc == DC - 1))
                        last.then_inc(half_full, 1)

                    def turn(t, k, grp):
                        bank, free, full = ((ps_ta, ta_free, ta_full), (ps_td, td_free, td_full))[grp % 2]
                        pe.wait_ge(free, 2 * t + grp // 2 + 1)
                        for n in range(GRP):
                            j = GRP * grp + n
                            last = nc.tensor.transpose(bank[:, n * P:(n + 1) * P], probs[:, k, j * P:(j + 1) * P],
                                                       ident[:])
                        last.then_inc(full, 1)

                    for half in range(2):
                        scores(0, 0, half)

                    def tile_body(t, k, more):
                        if more:
                            scores(t + 1, 1 - k, 0)
                        pe.wait_ge(exped, t + 1)
                        turn(t, k, 0)
                        turn(t, k, 1)
                        if more:
                            scores(t + 1, 1 - k, 1)
                        turn(t, k, 2)
                        turn(t, k, 3)
                        pe.wait_ge(added, t + 1)
                        pe.wait_ge(ta_free, 2 * t + 3)
                        pe.wait_ge(td_free, 2 * t + 3)
                        for j in range(NT):
                            last = nc.tensor.matmul(ps_o[:, k, 0:D], probs_t[:, k, j, :], support[:, j, :],
                                                    start=(j == 0), stop=(j == NT - 1))
                        last.then_inc(pv_done, 1)

                    each_tile(pe, tile_body)

                @block.scalar
                def _(act):
                    act.sem_inc(proj_free, 2)
                    act.sem_inc(ta_free, 1)
                    take_root(act, squared_ready, root_ready, 1)
                    normalise(act, stats_ready, h, h_ready)
                    for n in range(4):
                        oc, half = n // 2, n % 2
                        act.wait_ge(proj_full, n + 1)
                        nc.scalar.activation(eT[:, oc, half * HALF:(half + 1) * HALF], ps_s[:, half, :], ACT.Copy)\
                            .then_inc(proj_free, 1)
                    for n in range(4):
                        act.wait_ge(proj_full, 4 + n + 1)
                        nc.scalar.activation(support[:, 4 * n:4 * n + 4, :],
                                             ps_s[:, n % 2, :].rearrange("p (t d) -> p t d", d=D), ACT.Copy)\
                            .then_inc(proj_free, 1)
                    act.wait_ge(neg_ready, 1)
                    nc.scalar.activation(node_att[:], logits[:], ACT.Exp, bias=node_max[:, 2:3],
                                         accum_out=node_sum[:, 0:1]).then_inc(node_exp, 1)

                    def exponentials(t, k):
                        act.wait_ge(masked, t + 3)
                        nc.scalar.activation(probs[:, k, :], probs[:, k, :], ACT.Exp, bias=neg_max[:, k:k + 1],
                                             accum_out=den[:, k:k + 1]).then_inc(exped, 1)

                    exponentials(0, 0)

                    def tile_body(t, k, more):
                        act.wait_ge(pv_done, t + 1)
                        for n in range(2):
                            act.wait_ge(ta_full, 2 * t + n + 1)
                            nc.scalar.activation(probs_t[:, k, 2 * GRP * n:2 * GRP * n + GRP, :],
                                                 ps_ta[:].rearrange("p (j q) -> p j q", q=P), ACT.Copy)\
                                .then_inc(ta_free, 1)
                        if more:
                            exponentials(t + 1, 1 - k)

                    each_tile(act, tile_body)

                @block.vector
                def _(dve):
                    dve.sem_inc(half_free, 2)
                    dve.sem_inc(masked, 2)
                    dve.sem_inc(td_free, 1)
                    dve.sem_inc(added, 2)
                    link = chained(dve, steps)
                    norm_statistics(dve, link, squared_ready, root_ready, 1)
                    dve.sem_inc(stats_ready, 1)
                    store_turned(dve, hT, ps_rows, turned, evacuated)
                    dve.wait_ge(w_in, 4 * 16)
                    for t in range(NT):
                        last = nc.vector.tensor_tensor_reduce(products[:, t, :], h[:, t, :], node_rows[:], 1.0, 0.0,
                                                              ALU.mult, ALU.add, logits[:, t:t + 1])
                    link(last)
                    nc.vector.tensor_reduce(node_max[:, 0:1], logits[:], AX_X, ALU.max).then_inc(max_ready, 1)
                    dve.wait_ge(all_max, 1)
                    nc.vector.tensor_scalar(node_max[:, 2:3], node_max[:, 1:2], -1.0, None, ALU.mult)\
                        .then_inc(neg_ready, 1)
                    link(nc.vector.tensor_tensor(acc[:], acc[:], bias_rows[:].unsqueeze(1).to_broadcast([P, NT, D]),
                                                 ALU.add))
                    link(nc.vector.tensor_scalar(has_edge[:], deg[:], 1.0, None, ALU.min))
                    dve.wait_ge(all_sum, 1)
                    link(nc.vector.reciprocal(node_sum[:, 2:3], node_sum[:, 1:2]))
                    link(nc.vector.scalar_tensor_tensor(out=node_att[:], in0=node_att[:], scalar=node_sum[:, 2:3],
                                                        in1=has_edge[:], op0=ALU.mult, op1=ALU.mult))

                    def mask_half(t, k, half):
                        if half == 0:
                            dve.wait_ge(mask_in[k], 8 * t - 8 * k + 16)
                            nc.vector.tensor_copy(mask[:, k, bass.ds(t * P, P)],
                                                  mask_diag[:, bass.ds(t, 1), :].rearrange("p t q -> p (t q)"))\
                                .then_inc(mask_patched, 1)
                            dve.wait_ge(mask_patched, t + 1)
                            dve.wait_ge(td_full, 2 * t + 2)
                        dve.wait_ge(half_full, 2 * t + half + 5)
                        stand_alone(dve)
                        nc.vector.tensor_tensor_reduce(
                            probs[:, k, half * HALF:(half + 1) * HALF], ps_s[:, half, :],
                            mask[:, k, half * HALF:(half + 1) * HALF], 1.0, LOWEST, ALU.add, ALU.max,
                            row_max[:, k, half:half + 1]).then_inc(half_free, 1)

                    def finish_mask(t, k):
                        dve.wait_ge(half_free, 2 * t + 4)
                        nc.vector.tensor_reduce(neg_max[:, k:k + 1], row_max[:, k, :], AX_X, ALU.max, negate=True)\
                            .then_inc(masked, 1)

                    def copy_group(t, k, n):
                        dve.wait_ge(td_full, 2 * t + n + 5)
                        nc.vector.tensor_copy(probs_t[:, k, GRP + 2 * GRP * n:2 * GRP + 2 * GRP * n, :],
                                              ps_td[:].rearrange("p (j q) -> p j q", q=P)).then_inc(td_free, 1)

                    mask_half(0, 0, 0)
                    mask_half(0, 0, 1)
                    finish_mask(0, 0)

                    def tile_body(t, k, more):
                        dve.wait_ge(pv_done, t + 1)
                        if more:
                            mask_half(t + 1, 1 - k, 0)
                        copy_group(t, k, 0)
                        if more:
                            mask_half(t + 1, 1 - k, 1)
                            finish_mask(t + 1, 1 - k)
                        copy_group(t, k, 1)
                        nc.vector.reciprocal(rden[:, k:k + 1], den[:, k:k + 1]).then_inc(scale_steps, 1)
                        dve.wait_ge(scale_steps, 2 * t + 1)
                        scale = row_scale[:, bass.ds(t, 1)]
                        nc.vector.tensor_tensor(scale, rden[:, k:k + 1], node_att[:, bass.ds(t, 1)], ALU.mult)\
                            .then_inc(scale_steps, 1)
                        dve.wait_ge(scale_steps, 2 * t + 2)
                        dve.wait_ge(pv_done, t + 3)
                        rows = acc[:, bass.ds(t, 1), :].rearrange("p t d -> p (t d)")
                        nc.vector.scalar_tensor_tensor(out=rows, in0=ps_o[:, k, 0:D], scalar=scale, in1=rows,
                                                       op0=ALU.mult, op1=ALU.add).then_inc(added, 1)

                    each_tile(dve, tile_body)

    if stop >= 4:
        with ExitStack() as ctx:
            sb, ps, sem = allocators(ctx)
            w3_sb = sb("w3_sb", [P, DC, D], F32)
            w3_t = sb("w3_t", [P, DC, D], F32)
            b3_rows = sb("b3_rows", [P, D], F32)
            d_root = sb("d_root", [P, NT], F32)
            with_self = sb("with_self", [P, 2, D], F32)
            z = sb("z", [P, 2, D], F32)
            z_t = sb("z_t", [P, 2, DC, P], F32)
            linear = sb("linear", [P, 2, D], F32)
            h_parts = sb("h_parts3", [P, NT, 2, D], F16)
            ps_g = ps("ps_g3", [P, 2, 2 * D])
            ps_z = ps("ps_z", [P, 2, 512])
            ps_f = ps("ps_f", [P, 2, 512])

            w_in = sem("w_in3")
            steps, squared_ready, root_ready, stats_ready = (sem(f"{s}_3") for s in ("steps", "sq", "root", "stats"))
            h_ready, parts_ready = sem("h_ready3"), sem("parts_ready3")
            w3_turned, w3_ready = sem("w3_turned"), sem("w3_ready")
            gathered, z_steps, z_ready = sem("gathered3"), sem("z_steps"), sem("z_ready")
            z_turned, z_t_ready = sem("z_turned"), sem("z_t_ready")
            final_ready, linear_ready, rows_ready = sem("final_ready"), sem("linear_ready"), sem("rows_ready")
            stored = sem("stored")

            def each_round(eng, body):
                body(0, 0, False, False)
                with eng.Fori(0, NT // 2 - 1) as i:
                    body(2 * i + 1, 1, True, False)
                    body(2 * i + 2, 0, True, False)
                body(NT - 1, 1, True, False)
                body(NT, 0, True, True)

            with nc.Block() as block:
                @block.sync
                def _(sp):
                    sp.dma_start(w3_sb[:], W3.rearrange("(c p) i -> p c i", p=P)).then_inc(w_in, 16)
                    sp.dma_start(b3_rows[:], b3.partition_broadcast(P)).then_inc(w_in, 16)
                    with sp.Fori(0, NT) as t:
                        sp.wait_ge(rows_ready, t + 1)
                        sp.dma_start(out[bass.ds(t * P, P), :],
                                     acc[:, bass.ds(t, 1), :].rearrange("p t d -> p (t d)")).then_inc(stored, 16)
                    sp.wait_ge(stored, 16 * NT)

                @block.tensor
                def _(pe):
                    pe.wait_ge(w_in, 2 * 16)
                    for ic in range(DC):
                        for oc in range(DC):
                            last = nc.tensor.transpose(ps_z[:, ic, oc * P:(oc + 1) * P],
                                                       w3_sb[:, oc, ic * P:(ic + 1) * P], ident[:])
                    last.then_inc(w3_turned, 1)
                    pe.wait_ge(w3_ready, 1)
                    pe.wait_ge(parts_ready, NT)

                    def round_body(t, k, previous, only):
                        if not only:
                            gather(t, k, h_parts, ps_g, range(NT // 2))
                        if previous:
                            pe.wait_ge(z_ready, t)
                            for dc in range(DC):
                                last = nc.tensor.transpose(ps_z[:, 1 - k, dc * P:(dc + 1) * P],
                                                           z[:, 1 - k, dc * P:(dc + 1) * P], ident[:])
                            last.then_inc(z_turned, 1)
                        if not only:
                            gather(t, k, h_parts, ps_g, range(NT // 2, NT)).then_inc(gathered, 1)
                        if previous:
                            pe.wait_ge(z_t_ready, t)
                            for dc in range(DC):
                                last = nc.tensor.matmul(ps_f[:, 1 - k, 0:D], z_t[:, 1 - k, dc, :], w3_t[:, dc, :],
                                                        start=(dc == 0), stop=(dc == DC - 1))
                            last.then_inc(final_ready, 1)

                    each_round(pe, round_body)

                @block.scalar
                def _(act):
                    take_root(act, squared_ready, root_ready, 1)
                    take_root(act, squared_ready, root_ready, 2)
                    act.wait_ge(w3_turned, 1)
                    nc.scalar.activation(w3_t[:], ps_z[:, :, 0:D], ACT.Copy).then_inc(w3_ready, 1)
                    normalise(act, stats_ready, h, h_ready)

                    def round_body(t, k, previous, only):
                        if previous:
                            act.wait_ge(z_turned, t)
                            nc.scalar.activation(z_t[:, 1 - k], ps_z[:, 1 - k, 0:D]
                                                 .rearrange("p (c q) -> p c q", c=DC), ACT.Copy).then_inc(z_t_ready, 1)

                    each_round(act, round_body)

                @block.vector
                def _(dve):
                    link = chained(dve, steps)
                    link(nc.vector.tensor_scalar(squared[:], deg[:], 1.0, None, ALU.add))
                    inverse_root(dve, link, squared_ready, root_ready, 1)
                    link(nc.vector.tensor_copy(d_root[:], rstd[:]))
                    norm_statistics(dve, link, squared_ready, root_ready, 2)
                    link(nc.vector.tensor_tensor(rstd[:], rstd[:], d_root[:], ALU.mult))
                    nc.vector.tensor_tensor(nbias[:], nbias[:], d_root[:], ALU.mult).then_inc(stats_ready, 1)
                    dve.wait_ge(h_ready, NT)
                    split_rows(dve, h_parts, parts_ready)
                    dve.wait_ge(w_in, 2 * 16)

                    def round_body(t, k, previous, only):
                        if not only:
                            dve.wait_ge(gathered, t + 1)
                            nc.vector.tensor_tensor(with_self[:, k, :], ps_g[:, k, 0:D],
                                                    h[:, bass.ds(t, 1), :].rearrange("p t d -> p (t d)"), ALU.add)\
                                .then_inc(z_steps, 1)
                            dve.wait_ge(z_steps, t + 1)
                            nc.vector.tensor_tensor(z[:, k, :], ps_g[:, k, D:2 * D], with_self[:, k, :], ALU.add)\
                                .then_inc(z_ready, 1)
                        if previous:
                            dve.wait_ge(final_ready, t)
                            rows = acc[:, bass.ds(t - 1, 1), :].rearrange("p t d -> p (t d)")
                            nc.vector.scalar_tensor_tensor(out=linear[:, 1 - k, :], in0=ps_f[:, 1 - k, 0:D],
                                                           scalar=d_root[:, bass.ds(t - 1, 1)], in1=b3_rows[:],
                                                           op0=ALU.mult, op1=ALU.add).then_inc(linear_ready, 1)
                            dve.wait_ge(linear_ready, t)
                            nc.vector.scalar_tensor_tensor(out=rows, in0=linear[:, 1 - k, :], scalar=0.0, in1=rows,
                                                           op0=ALU.max, op1=ALU.add).then_inc(rows_ready, 1)

                    each_round(dve, round_body)
    else:
        with ExitStack() as ctx:
            _, _, sem = allocators(ctx)
            stored = sem("stored")
            with nc.Block() as block:
                @block.sync
                def _(sp):
                    sp.dma_start(out.rearrange("(t p) d -> p t d", p=P), acc[:]).then_inc(stored, 16)
                    sp.wait_ge(stored, 16)
    late.close()
    whole.close()


_INS = ['x', 'adj', 'L0_gnn_Wks', 'L0_gnn_Wqs', 'L0_gnn_Wvs', 'L0_gnn_Wo', 'L2_gnn_weight', 'L2_gnn_bias',
        'L2_gnn_node_w', 'L2_gnn_edge_w', 'L3_gnn_W', 'L3_gnn_b']


def kernel(**inputs):
    import numpy as _np
    import concourse.bacc as _bacc
    from concourse import mybir as _mybir
    from concourse.bass_utils import run_bass_kernel_spmd as _run

    nc = _bacc.Bacc("TRN2", target_bir_lowering=False, num_devices=1)
    arrays, args = {}, []
    for name in _INS:
        a = _np.ascontiguousarray(inputs[name])
        arrays[f"in_{name}_dram"] = a
        args.append(nc.dram_tensor(f"in_{name}_dram", a.shape, _mybir.dt.from_np(a.dtype), kind="ExternalInput").ap())
    args.append(nc.dram_tensor("out_dram", (N, D), F32, kind="ExternalOutput").ap())
    program(nc, *args)
    r = _run(nc, [arrays], core_ids=[0])
    return r.results[0]["out_dram"]
```

```python
from contextlib import ExitStack

import concourse.bass as bass
from concourse import mybir

F32 = mybir.dt.float32
F16 = mybir.dt.float16
BF16 = mybir.dt.bfloat16
F8 = mybir.dt.float8e4
U16 = mybir.dt.uint16
ALU = mybir.AluOpType
ACT = mybir.ActivationFunctionType
AX_X = mybir.AxisListType.X
RMAX = bass.bass_isa.ReduceOp.max
RADD = bass.bass_isa.ReduceOp.add

P = 128
N = 2048
D = 256
NT = N // P
DC = D // P
H = 8
KD = 64
PAIRS = H // 2
NCH = NT // 2
CQ = 2 * P
UPC = 4
UPP = NCH * UPC
HALF = N // 2
AHEAD = 2
HPP = 6 + 2 * UPP
Q_HALF, K_HALF, V_HALF = 0, 2, 6
GRP = 4
BIG = 2.0 ** 53
IDENTITY_BIAS = 0.01
LN_EPS = 1e-5
NORM_EPS = 1e-12
LOWEST = -3.0e38



def program(nc, x, adj, Wks, Wqs, Wvs, Wo, weight, bias, node_w, edge_w, W3, b3, out, stop=9):
    mask_dram = nc.dram_tensor("mask_rows", (NT, P, N), BF16).ap()
    diag_dram = nc.dram_tensor("mask_diagonals", (P, NT, P), BF16).ap()

    def allocators(ctx):
        def sb(name, shape, dt):
            return ctx.enter_context(nc.sbuf_tensor(name, shape, dt))

        def ps(name, shape, dt=F32):
            return ctx.enter_context(nc.psum_tensor(name, shape, dt))

        def sem(name):
            return ctx.enter_context(nc.semaphore(name))
        return sb, ps, sem

    whole = ExitStack()
    sb, _, _ = allocators(whole)
    acc = sb("acc", [P, NT, D], F32)
    ident = sb("ident", [P, P], F32)
    bias_eye = sb("bias_eye", [P, P], F32)
    deg = sb("deg", [P, NT], F32)
    adjt = sb("adjt", [P, NT, NT, P], F8)
    rstd = sb("rstd", [P, NT], F32)
    nbias = sb("nbias", [P, NT], F32)
    squared = sb("squared", [P, NT], F32)
    root = sb("root", [P, NT], F32)
    tmp = sb("tmp", [P, NT], F32)

    def stand_alone(eng):
        eng.nop(nofuse=True)

    def chained(eng, sem):
        count = [0]

        def link(ins):
            count[0] += 1
            ins.then_inc(sem, 1)
            eng.wait_ge(sem, count[0])
        return link

    def inverse_root(dve, link, squared_ready, root_ready, n):
        dve.sem_inc(squared_ready, 1)
        dve.wait_ge(root_ready, n)
        link(nc.vector.reciprocal(rstd[:], root[:]))
        link(nc.vector.tensor_tensor(tmp[:], rstd[:], rstd[:], ALU.mult))
        link(nc.vector.tensor_tensor(tmp[:], tmp[:], squared[:], ALU.mult))
        link(nc.vector.tensor_scalar(tmp[:], tmp[:], -0.5, 1.5, ALU.mult, ALU.add))
        link(nc.vector.tensor_tensor(rstd[:], rstd[:], tmp[:], ALU.mult))

    def norm_statistics(dve, link, moments, squared_ready, root_ready, n):
        stats, meanvar = moments[:, :, 0:6], moments[:, :, 6:8]
        for t in range(NT):
            last = nc.vector.bn_stats(stats[:, t, :], acc[:, t, :])
        link(last)
        for t in range(NT):
            last = nc.vector.bn_aggr(meanvar[:, t, :], stats[:, t, :])
        link(last)
        link(nc.vector.tensor_scalar(squared[:], meanvar[:, :, 1], LN_EPS, None, ALU.add))
        inverse_root(dve, link, squared_ready, root_ready, n)
        link(nc.vector.scalar_tensor_tensor(out=nbias[:], in0=meanvar[:, :, 0], scalar=-1.0, in1=rstd[:],
                                            op0=ALU.mult, op1=ALU.mult))

    def take_root(act, squared_ready, root_ready, n):
        act.wait_ge(squared_ready, n)
        nc.scalar.activation(root[:], squared[:], ACT.Sqrt).then_inc(root_ready, 1)

    def normalise(act, stats_ready, h, h_ready):
        act.wait_ge(stats_ready, 1)
        for t in range(NT):
            nc.scalar.activation(h[:, t, :], acc[:, t, :], ACT.Relu, bias=nbias[:, t:t + 1],
                                 scale=rstd[:, t:t + 1]).then_inc(h_ready, 1)

    def turn_rows(pe, h, h_ready, ps_rows, turned, evacuated):
        for g in range(NT // 2):
            pe.wait_ge(h_ready, 2 * g + 2)
            if g >= 2:
                pe.wait_ge(evacuated, g - 1)
            for dc in range(DC):
                for k in range(2):
                    last = nc.tensor.transpose(ps_rows[:, g % 2, dc, k * P:(k + 1) * P],
                                               h[:, 2 * g + k, dc * P:(dc + 1) * P], ident[:])
            last.then_inc(turned, 1)

    def store_turned(dve, hT, ps_rows, turned, evacuated):
        for g in range(NT // 2):
            dve.wait_ge(turned, g + 1)
            nc.vector.tensor_copy(hT[:, :, g * 2 * P:(g + 1) * 2 * P], ps_rows[:, g % 2])\
                .then_inc(evacuated, 1)

    layer0 = ExitStack()
    sb0, ps0, sem0 = allocators(layer0)
    hT = sb0("hT", [P, DC, N], F32)
    w_pair = sb0("w_pair", [P, 3, DC, 2 * KD], F32)
    q_parts = sb0("q_parts", [P, 2, N], F16)
    k_parts = sb0("k_parts", [P, 2, 2, N], F16)
    mask = sb0("mask", [P, 2, N], BF16)
    ps_s = ps0("ps_s", [P, 2, HALF])

    w_in = sem0("w_in")
    half_full = sem0("half_full")
    half_free = sem0("half_free")
    hi_ready = sem0("hi_ready")
    k_doubled = [sem0(f"k_doubled{half}") for half in range(2)]

    def load_pair(pool, pair):
        for n, w in enumerate((Wqs, Wks, Wvs)):
            for a in range(2):
                pool.dma_start(w_pair[:, n, :, a * KD:(a + 1) * KD],
                               w[bass.ds(2 * pair + a, 1)].rearrange("h (c p) k -> p (h c) k", p=P))\
                    .then_inc(w_in, 16)

    def free_half(pe, pair, n):
        pe.wait_ge(half_free, HPP * pair + n + 1)

    def project(pe, pair, n, half):
        if half == 0 and n == 0:
            pe.wait_ge(w_in, 6 * 16 * (pair + 1))
        free_half(pe, pair, 2 * n + half)
        for c in range(2):
            for dc in range(DC):
                first = half * HALF + c * 512
                last = nc.tensor.matmul(ps_s[:, half, c * 512:(c + 1) * 512], w_pair[:, n, dc, :],
                                        hT[:, dc, first:first + 512], start=(dc == 0), stop=(dc == DC - 1))
        last.then_inc(half_full, 1)

    def hi_parts(act, pair, n, half):
        act.wait_ge(half_full, HPP * pair + 2 * n + half + 1)
        cols = slice(half * HALF, (half + 1) * HALF)
        for a in range(2):
            hi = (q_parts[0:KD, a, cols], k_parts[0:KD, a, 0, cols])[n]
            last = nc.scalar.activation(hi, ps_s[a * KD:(a + 1) * KD, half, :], ACT.Copy, scale=(KD ** -0.5, 1.0)[n])
        last.then_inc(hi_ready, 1)

    def lo_parts(dve, pair, n, half):
        dve.wait_ge(hi_ready, 4 * pair + 2 * n + half + 1)
        cols = slice(half * HALF, (half + 1) * HALF)
        for a in range(2):
            if n == 0:
                hi, lo = q_parts[0:KD, a, cols], q_parts[KD:P, a, cols]
            else:
                hi, lo = k_parts[0:KD, a, 0, cols], k_parts[0:KD, a, 1, cols]
            last = nc.vector.scalar_tensor_tensor(out=lo, in0=ps_s[a * KD:(a + 1) * KD, half, :],
                                                  scalar=(KD ** -0.5, 1.0)[n], in1=hi,
                                                  op0=ALU.mult, op1=ALU.subtract)
        last.then_inc(half_free, 1)

    def double_k(sp, pair):
        for half in range(2):
            sp.wait_ge(half_free, HPP * pair + K_HALF + half + 3)
            cols = slice(half * HALF, (half + 1) * HALF)
            sp.dma_start(k_parts[KD:P, :, :, cols], k_parts[0:KD, :, :, cols]).then_inc(k_doubled[half], 16)

    with ExitStack() as ctx:
        sb, ps, sem = allocators(ctx)
        h = sb("h_in", [P, NT, D], F32)
        moments = sb("moments_in", [P, NT, 8], F32)
        ident16 = sb("ident16", [P, P], F16)
        not_eye = sb("not_eye", [P, P], BF16)
        mask_diag = sb("mask_diag", [P, NT, P], BF16)
        adj_in = sb("adj_in", [P, 4, N], F32)
        adj16 = sb("adj16", [P, 2, N], F16)
        ps_adjt = ps("ps_adjt", [P, 2, N], F16)
        ps_rows = ps_s[:, :, 0:512].rearrange("p b (c q) -> p b c q", c=DC)

        x_in = sem("x_in")
        adj_loaded = [sem(f"adj_loaded{k}") for k in range(4)]
        filled, consts = sem("consts_filled"), sem("consts_ready")
        steps, squared_ready, root_ready, stats_ready = (sem(f"{s}_in") for s in ("steps", "sq", "root", "stats"))
        h_ready, turned, evacuated = (sem(f"{s}_in") for s in ("h_ready", "turned", "evacuated"))
        adj_copied = sem("adj_copied")
        mask_written = sem("mask_written")
        masked = sem("masked_in")
        adj_turned = sem("adj_turned")
        adjt_stored = sem("adjt_stored")
        mask_out = [sem(f"mask_out{k}") for k in range(2)]
        diag_out = sem("diag_out")

        def interleaved(eng, tile, norm, part, unrolled=False):
            for t in range(4):
                tile(t, t)
            norm()
            for n in range(2):
                for half in range(2):
                    part(n, half)
                    tile(4 + 2 * n + half, 2 * n + half)
            if unrolled:
                for t in range(8, NT):
                    tile(t, t % 4)
            else:
                with eng.Fori(2, NT // 4) as i:
                    for k in range(4):
                        tile(4 * i + k, k)

        with nc.Block() as block:
            @block.sync
            def _(sp):
                for k in range(2):
                    sp.sem_inc(mask_out[k], 16)

                def load(t, k):
                    sp.wait_ge(adj_copied, t + 1)
                    sp.dma_start(adj_in[:, k, :], adj[bass.ds(t * P, P), :]).then_inc(adj_loaded[k], 16)

                def store_mask(t, k):
                    sp.wait_ge(masked, t + 3)
                    sp.dma_start(mask_dram[t], mask[:, k, :]).then_inc(mask_out[k], 16)

                sp.dma_start(acc[:], x.rearrange("(t p) d -> p t d", p=P)).then_inc(x_in, 16)
                for t in range(4):
                    load(t, t)
                with sp.Fori(1, NT // 4) as i:
                    for k in range(4):
                        load(4 * i + k, k)
                        store_mask(4 * i + k - 4, k % 2)
                double_k(sp, 0)
                for t in range(NT - 4, NT):
                    store_mask(t, t % 2)
                sp.dma_start(diag_dram, mask_diag[:]).then_inc(diag_out, 16)
                for k in range(2):
                    sp.wait_ge(mask_out[k], 16 * NT // 2 + 16)
                sp.wait_ge(diag_out, 16)

            @block.gpsimd
            def _(pool):
                load_pair(pool, 0)
                nc.gpsimd.memset(ident[:], 0.0).then_inc(filled, 1)
                nc.gpsimd.memset(ident16[:], 0.0).then_inc(filled, 1)
                nc.gpsimd.memset(bias_eye[:], 0.0).then_inc(filled, 1)
                nc.gpsimd.memset(not_eye[:], 1.0).then_inc(filled, 1)
                pool.wait_ge(filled, 4)
                for m, v in ((ident, 1.0), (ident16, 1.0), (bias_eye, IDENTITY_BIAS), (not_eye, 0.0)):
                    nc.gpsimd.affine_select(out=m[:], in_=m[:], compare_op=ALU.not_equal, fill=v, base=0,
                                            pattern=[[-1, P]], channel_multiplier=1).then_inc(consts, 1)
                pool.sem_inc(masked, 2)
                pool.wait_ge(consts, 4)

                def mask_tile(t, k):
                    pool.wait_ge(adj_copied, t + 5)
                    pool.wait_ge(mask_out[k], 8 * (t - k) + 16)
                    stand_alone(pool)
                    nc.gpsimd.tensor_scalar(mask[:, k, :], adj16[:, k, :], -1.0, BIG, ALU.add, ALU.mult)\
                        .then_inc(mask_written, 1)
                    pool.wait_ge(mask_written, 2 * t + 1)
                    diag = mask[:, k, bass.ds(t * P, P)]
                    nc.gpsimd.tensor_copy(mask_diag[:, bass.ds(t, 1), :].rearrange("p t q -> p (t q)"), diag)\
                        .then_inc(mask_written, 1)
                    pool.wait_ge(mask_written, 2 * t + 2)
                    stand_alone(pool)
                    nc.gpsimd.tensor_tensor(diag, diag, not_eye[:], ALU.mult).then_inc(masked, 1)

                with pool.Fori(0, NT // 2) as i:
                    for k in range(2):
                        mask_tile(2 * i + k, k)

            @block.scalar
            def _(act):
                act.sem_inc(adj_copied, 4)

                def copy_tile(t, slot):
                    k = slot % 2
                    act.wait_ge(adj_loaded[slot], 4 * (t - slot) + 16)
                    act.wait_ge(adj_turned, t + 1)
                    act.wait_ge(masked, t + 1)
                    nc.scalar.activation(adj16[:, k, :], adj_in[:, slot, :], ACT.Copy,
                                         accum_out=deg[:, bass.ds(t, 1)]).then_inc(adj_copied, 1)

                def norm():
                    take_root(act, squared_ready, root_ready, 1)
                    normalise(act, stats_ready, h, h_ready)

                interleaved(act, copy_tile, norm, lambda n, half: hi_parts(act, 0, n, half))

            @block.tensor
            def _(pe):
                pe.sem_inc(adj_turned, 2)
                pe.wait_ge(consts, 4)

                def turn_tile(t, slot):
                    k = slot % 2
                    pe.wait_ge(adj_copied, t + 5)
                    pe.wait_ge(adjt_stored, t + 1)
                    for j in range(NT):
                        last = nc.tensor.transpose(ps_adjt[:, k, j * P:(j + 1) * P],
                                                   adj16[:, k, j * P:(j + 1) * P], ident16[:])
                    last.then_inc(adj_turned, 1)

                def norm():
                    turn_rows(pe, h, h_ready, ps_rows, turned, evacuated)
                    pe.wait_ge(evacuated, NT // 2)

                interleaved(pe, turn_tile, norm, lambda n, half: project(pe, 0, n, half))

            @block.vector
            def _(dve):
                dve.sem_inc(adjt_stored, 2)
                dve.sem_inc(half_free, 2)
                link = chained(dve, steps)
                dve.wait_ge(x_in, 16)
                norm_statistics(dve, link, moments, squared_ready, root_ready, 1)
                dve.sem_inc(stats_ready, 1)

                def store_tile(t, slot):
                    dve.wait_ge(adj_turned, t + 3)
                    nc.vector.tensor_copy(adjt[:, t].rearrange("p j q -> p (j q)"),
                                          ps_adjt[:, slot % 2, :], saturate=False).then_inc(adjt_stored, 1)

                interleaved(dve, store_tile, lambda: store_turned(dve, hT, ps_rows, turned, evacuated),
                            lambda n, half: lo_parts(dve, 0, n, half), unrolled=True)

    if stop >= 1:
        with ExitStack() as ctx:
            sb, ps, sem = allocators(ctx)
            wo_sb = sb("wo_sb", [P, D], F32)
            v_sb = sb("v_sb", [P, NT, 2 * KD], F32)
            probs = sb("probs", [P, UPC, N], F32)
            probs_t = sb("probs_t", [P, 2, 2, NT, CQ], F32)
            row_max = sb("row_max", [P, UPC, 2], F32)
            neg_max = sb("neg_max", [P, UPC], F32)
            den = sb("den", [P, 2, UPC], F32)
            rden = sb("rden", [P, UPC], F32)
            rden_rows = sb("rden_rows", [P, UPC, KD], F32)
            o_normed = sb("o_normed", [P, CQ], F32)
            ps_ta = ps("ps_ta", [P, GRP * P])
            ps_td = ps("ps_td", [P, GRP * P])
            ps_o = ps("ps_o", [P, 512])
            ps_x = ps("ps_x", [P, 512])

            wo_in = sem("wo_in")
            mask_in = [sem(f"mask_in{k}") for k in range(2)]
            masked = sem("masked")
            exped = sem("exped")
            ta_full, ta_free = sem("ta_full"), sem("ta_free")
            td_full, td_free = sem("td_full"), sem("td_free")
            pv_done = sem("pv_done")
            rden_ready = sem("rden_ready")
            rden_turned = sem("rden_turned")
            rden_t_ready = sem("rden_t_ready")
            o_ready = sem("o_ready")
            out_ready = sem("out_ready")
            added = sem("added")
            steps = sem("steps0")

            def half_of(u, half):
                return 4 + half if isinstance(u, int) and u == 0 else 6 + 2 * u + half

            def each_chunk(eng, body):
                body(0, 0, True, False)
                with eng.Fori(0, (NCH - 2) // 2) as i:
                    body(2 * i + 1, 1, False, False)
                    body(2 * i + 2, 0, False, False)
                body(NCH - 1, 1, False, True)

            def each_pair(eng, body):
                with eng.Fori(0, PAIRS - 1) as pair:
                    body(pair, False)
                body(PAIRS - 1, True)

            with nc.Block() as block:
                @block.sync
                def _(sp):
                    def load_masks(pair, c):
                        for k in range(2):
                            sp.wait_ge(masked, UPP * pair + UPC * c + 2 * k + 2)
                            sp.dma_start(mask[:, k, :], mask_dram[2 * c + k]).then_inc(mask_in[k], 16)

                    load_masks(0, 0)
                    with sp.Fori(1, NCH) as c:
                        load_masks(0, c)
                    with sp.Fori(1, PAIRS) as pair:
                        load_masks(pair, 0)
                        double_k(sp, pair)
                        with sp.Fori(1, NCH) as c:
                            load_masks(pair, c)

                @block.gpsimd
                def _(pool):
                    def load_wo(pair):
                        pool.dma_start(wo_sb[:], Wo[bass.ds(2 * pair, 2)].rearrange("a k o -> (a k) o"))\
                            .then_inc(wo_in, 16)

                    load_wo(0)
                    with pool.Fori(1, PAIRS) as pair:
                        pool.wait_ge(half_full, HPP * (pair - 1) + V_HALF + 2)
                        stand_alone(pool)
                        load_pair(pool, pair)
                        pool.wait_ge(out_ready, NCH * pair)
                        stand_alone(pool)
                        load_wo(pair)

                @block.tensor
                def _(pe):
                    pe.sem_inc(td_full, 8)
                    pe.sem_inc(pv_done, 2)

                    def project_v(pair, half):
                        free_half(pe, pair, V_HALF + half)
                        for t in range(NT // 2):
                            for dc in range(DC):
                                first = (half * NT // 2 + t) * P
                                last = nc.tensor.matmul(ps_s[:, half, t * P:(t + 1) * P],
                                                        hT[:, dc, first:first + P], w_pair[:, 2, dc, :],
                                                        start=(dc == 0), stop=(dc == DC - 1))
                        last.then_inc(half_full, 1)

                    def scores(pair, u, q_tile, head, half):
                        free_half(pe, pair, half_of(u, half))
                        for n in range(2):
                            cols = slice(half * HALF + n * 512, half * HALF + (n + 1) * 512)
                            for part in range(2):
                                last = nc.tensor.matmul(ps_s[:, half, n * 512:(n + 1) * 512],
                                                        q_parts[:, head, bass.ds(q_tile * P, P)],
                                                        k_parts[:, head, part, cols],
                                                        start=(part == 0), stop=(part == 1))
                        last.then_inc(half_full, 1)

                    def turn(g, w, grp):
                        bank, free, full = ((ps_ta, ta_free, ta_full), (ps_td, td_free, td_full))[grp % 2]
                        pe.wait_ge(free, 2 * g + grp // 2 + 1)
                        for k in range(GRP):
                            j = GRP * grp + k
                            last = nc.tensor.transpose(bank[:, k * P:(k + 1) * P],
                                                       probs[:, w, j * P:(j + 1) * P], ident[:])
                        last.then_inc(full, 1)

                    def attend(chunk, parity, js):
                        if js[0] == 0:
                            pe.wait_ge(ta_free, 2 * UPC * (chunk + 1) + 1)
                            pe.wait_ge(td_free, 2 * UPC * (chunk + 1) + 1)
                            pe.wait_ge(o_ready, chunk + 1)
                        for j in js:
                            for a in range(2):
                                last = nc.tensor.matmul(ps_o[a * KD:(a + 1) * KD, 0:CQ],
                                                        v_sb[:, j, a * KD:(a + 1) * KD],
                                                        probs_t[:, parity, a, j, :],
                                                        start=(j == 0), stop=(j == NT - 1),
                                                        skip_group_check=True)
                        if js[-1] == NT - 1:
                            last.then_inc(pv_done, 1)

                    def turn_rden(chunk):
                        pe.wait_ge(rden_ready, chunk + 1)
                        pe.wait_ge(added, chunk + 1)
                        for k in range(2):
                            last = nc.tensor.transpose(ps_x[:, k * P:(k + 1) * P],
                                                       rden_rows[:, 2 * k:2 * k + 2, :]
                                                       .rearrange("p a k -> p (a k)"), ident[:])
                        last.then_inc(rden_turned, 1)

                    def project_out(chunk, pair):
                        pe.wait_ge(wo_in, 16 * (pair + 1))
                        pe.wait_ge(o_ready, chunk + 2)
                        for k in range(2):
                            last = nc.tensor.matmul(ps_x[:, k * D:(k + 1) * D], o_normed[:, k * P:(k + 1) * P],
                                                    wo_sb[:], start=True, stop=True)
                        last.then_inc(out_ready, 1)

                    def first_scores(pair):
                        for half in range(2):
                            pe.wait_ge(k_doubled[half], 16 * (pair + 1))
                            scores(pair, 0, 0, 0, half)

                    def v_and_second_scores(pair):
                        for half in range(2):
                            project_v(pair, half)
                        for half in range(2):
                            scores(pair, 1, 0, 1, half)

                    first_scores(0)
                    v_and_second_scores(0)

                    def pair_body(pair, last_pair):
                        def chunk_body(c, parity, first, last_chunk):
                            chunk = NCH * pair + c
                            for w in range(UPC):
                                g = UPC * chunk + w

                                def run_ahead(half):
                                    if not last_chunk or w < UPC - AHEAD:
                                        scores(pair, UPC * c + w + AHEAD, 2 * c + (w + AHEAD) // 2, w % 2, half)
                                    elif not last_pair:
                                        project(pe, pair + 1, w - (UPC - AHEAD), half)

                                run_ahead(0)
                                pe.wait_ge(exped, g + 1)
                                turn(g, w, 0)
                                turn(g, w, 1)
                                if w == 3 and not first:
                                    attend(chunk - 1, 1 - parity, range(14, NT))
                                run_ahead(1)
                                turn(g, w, 2)
                                turn(g, w, 3)
                                if not first:
                                    if w < 3:
                                        attend(chunk - 1, 1 - parity, (range(0, 5), range(5, 10), range(10, 14))[w])
                                    if w == 1:
                                        turn_rden(chunk - 1)
                                    if w == 3:
                                        project_out(chunk - 1, pair)

                        each_chunk(pe, chunk_body)
                        final = NCH * pair + NCH - 1
                        attend(final, 1, range(0, 4))
                        turn_rden(final)
                        attend(final, 1, range(4, NT))
                        if not last_pair:
                            first_scores(pair + 1)
                        project_out(final, pair)
                        if not last_pair:
                            v_and_second_scores(pair + 1)

                    each_pair(pe, pair_body)

                @block.scalar
                def _(act):
                    act.sem_inc(ta_free, 1)

                    def exponentials(g, w, parity):
                        act.wait_ge(masked, g + UPC + 1)
                        nc.scalar.activation(probs[:, w, :], probs[:, w, :], ACT.Exp, bias=neg_max[:, w:w + 1],
                                             accum_out=den[:, parity, w:w + 1]).then_inc(exped, 1)

                    def copy_group(g, w, parity, k):
                        act.wait_ge(ta_full, 2 * g + k + 1)
                        first_j = 2 * GRP * k
                        nc.scalar.activation(
                            probs_t[:, parity, w % 2, first_j:first_j + GRP, w // 2 * P:(w // 2 + 1) * P],
                            ps_ta[:].rearrange("p (j q) -> p j q", q=P), ACT.Copy).then_inc(ta_free, 1)

                    def copy_rden(chunk):
                        act.wait_ge(rden_turned, chunk + 1)
                        nc.scalar.activation(o_normed[:], ps_x[:, 0:CQ], ACT.Copy).then_inc(rden_t_ready, 1)

                    for w in range(AHEAD):
                        exponentials(w, w, 0)

                    def pair_body(pair, last_pair):
                        def chunk_body(c, parity, first, last_chunk):
                            chunk = NCH * pair + c
                            act.wait_ge(pv_done, chunk + 1)
                            for w in range(UPC):
                                g = UPC * chunk + w
                                ahead = not last_chunk or w < UPC - AHEAD
                                if w == 2 and not first:
                                    copy_rden(chunk - 1)
                                for k in range(2):
                                    if not ahead and not last_pair:
                                        hi_parts(act, pair + 1, w - (UPC - AHEAD), k)
                                    copy_group(g, w, parity, k)
                                if ahead:
                                    exponentials(g + AHEAD, (w + AHEAD) % UPC, (parity + (w + AHEAD) // UPC) % 2)

                        each_chunk(act, chunk_body)
                        copy_rden(NCH * pair + NCH - 1)
                        if not last_pair:
                            for w in range(AHEAD):
                                exponentials(UPP * (pair + 1) + w, w, 0)

                    each_pair(act, pair_body)

                @block.vector
                def _(dve):
                    dve.sem_inc(masked, 4)
                    dve.sem_inc(td_free, 1)
                    dve.sem_inc(o_ready, 1)
                    dve.sem_inc(added, 1)

                    def copy_v(pair):
                        for half in range(2):
                            dve.wait_ge(half_full, HPP * pair + V_HALF + half + 1)
                            nc.vector.tensor_copy(v_sb[:, half * NT // 2:(half + 1) * NT // 2, :],
                                                  ps_s[:, half, :].rearrange("p (t k) -> p t k", k=2 * KD))\
                                .then_inc(half_free, 1)

                    def mask_half(pair, u, w, half):
                        dve.wait_ge(half_full, HPP * pair + half_of(u, half) + 1)
                        if half == 0:
                            dve.wait_ge(td_full, 2 * (UPP * pair + u) + 2)
                        stand_alone(dve)
                        nc.vector.tensor_tensor_reduce(
                            probs[:, w, half * HALF:(half + 1) * HALF], ps_s[:, half, :],
                            mask[:, w // 2, half * HALF:(half + 1) * HALF], 1.0, LOWEST, ALU.add, ALU.max,
                            row_max[:, w, half:half + 1]).then_inc(half_free, 1)

                    def finish_mask(pair, u, w, q_tile):
                        dve.wait_ge(half_free, HPP * pair + half_of(u, 1) + 3)
                        nc.vector.tensor_reduce(neg_max[:, w:w + 1], row_max[:, w, :], AX_X, ALU.max, negate=True)
                        diag = probs[:, w, bass.ds(q_tile * P, P)]
                        nc.vector.tensor_tensor(diag, diag, bias_eye[:], ALU.add).then_inc(masked, 1)

                    def mask_unit(pair, w):
                        dve.wait_ge(mask_in[0], 16 * NCH * pair + 16)
                        for half in range(2):
                            mask_half(pair, w, w, half)
                        finish_mask(pair, w, w, 0)

                    def copy_group(g, w, parity, k):
                        dve.wait_ge(td_full, 2 * g + k + 9)
                        first_j = GRP + 2 * GRP * k
                        nc.vector.tensor_copy(
                            probs_t[:, parity, w % 2, first_j:first_j + GRP, w // 2 * P:(w // 2 + 1) * P],
                            ps_td[:].rearrange("p (j q) -> p j q", q=P)).then_inc(td_free, 1)

                    def spread_rden(chunk, parity):
                        nc.vector.reciprocal(rden[:], den[:, parity, :]).then_inc(steps, 1)
                        dve.wait_ge(steps, chunk + 1)
                        nc.vector.tensor_copy(rden_rows[:], rden[:].unsqueeze(2).to_broadcast([P, UPC, KD]))\
                            .then_inc(rden_ready, 1)

                    def normalise_out(chunk):
                        dve.wait_ge(pv_done, chunk + 3)
                        dve.wait_ge(rden_t_ready, chunk + 1)
                        nc.vector.tensor_tensor(o_normed[:], ps_o[:, 0:CQ], o_normed[:], ALU.mult).then_inc(o_ready, 1)

                    def add_out(chunk, c):
                        dve.wait_ge(out_ready, chunk + 1)
                        rows = acc[:, bass.ds(2 * c, 2), :]
                        nc.vector.tensor_tensor(rows, ps_x[:].rearrange("p (t d) -> p t d", d=D), rows, ALU.add)\
                            .then_inc(added, 1)

                    mask_unit(0, 0)
                    copy_v(0)
                    mask_unit(0, 1)

                    def pair_body(pair, last_pair):
                        def chunk_body(c, parity, first, last_chunk):
                            chunk = NCH * pair + c
                            dve.wait_ge(pv_done, chunk + 1)
                            for w in range(UPC):
                                g = UPC * chunk + w
                                ahead = not last_chunk or w < UPC - AHEAD
                                u2, w2 = UPC * c + w + AHEAD, (w + AHEAD) % UPC
                                if w == 0 and not first:
                                    spread_rden(chunk - 1, 1 - parity)
                                if ahead and w2 % 2 == 0:
                                    dve.wait_ge(mask_in[w2 // 2], 16 * (chunk + (w + AHEAD) // UPC) + 16)
                                for k in range(2):
                                    if ahead:
                                        mask_half(pair, u2, w2, k)
                                    elif not last_pair:
                                        lo_parts(dve, pair + 1, w - (UPC - AHEAD), k)
                                    if ahead and k == 1:
                                        finish_mask(pair, u2, w2, 2 * c + (w + AHEAD) // 2)
                                    copy_group(g, w, parity, k)
                                    if w == 3 and k == 0 and not first:
                                        normalise_out(chunk - 1)
                                if w == 3 and not first:
                                    add_out(chunk - 1, c - 1)

                        each_chunk(dve, chunk_body)
                        final = NCH * pair + NCH - 1
                        spread_rden(final, 1)
                        normalise_out(final)
                        if not last_pair:
                            mask_unit(pair + 1, 0)
                        add_out(final, NCH - 1)
                        if not last_pair:
                            copy_v(pair + 1)
                            mask_unit(pair + 1, 1)

                    each_pair(dve, pair_body)
    layer0.close()

    late = ExitStack()
    sb, _, _ = allocators(late)
    h = sb("h", [P, NT, D], F32)
    moments = sb("moments", [P, NT, 8], F32)
    row_scale = sb("row_scale", [P, NT], F32)

    def split_rows(dve, h_parts, parts_ready):
        for t in range(0, NT, 2):
            hi, lo = (h_parts[:, t:t + 2, k, :] for k in range(2))
            nc.vector.tensor_copy(hi, h[:, t:t + 2, :]).then_inc(parts_ready, 1)
            dve.wait_ge(parts_ready, t + 1)
            nc.vector.tensor_tensor(lo, h[:, t:t + 2, :], hi, ALU.subtract).then_inc(parts_ready, 1)

    def fetch_tile(eng, t, slot, done):
        eng.dma_start(slot.rearrange("p j q -> p (j q)").bitcast(U16),
                      adjt[:, bass.ds(t, 1)].rearrange("p t j q -> p (t j q)").bitcast(U16)).then_inc(done, 16)

    def gather(slot, h_parts, ps_g, js):
        for j in js:
            last = nc.tensor.matmul(ps_g, slot[:, j, :], h_parts[:, j].rearrange("p a d -> p (a d)"),
                                    start=(j == 0), stop=(j == NT - 1))
        return last

    if stop >= 2:
        with ExitStack() as ctx:
            sb, ps, sem = allocators(ctx)
            inv_norm = sb("inv_norm", [P, NT], F32)
            inc_scale = sb("inc_scale", [P, NT], F32)
            h_parts = sb("h_parts1", [P, NT, 2, D], F16)
            slots = sb("slots1", [P, 4, NT, P], F8)
            ps_g = ps("ps_g1", [P, 2, 2 * D])
            fetched = [sem(f"fetched1{k}") for k in range(4)]
            steps, squared_ready, root_ready, stats_ready = (sem(f"{s}_1") for s in ("steps", "sq", "root", "stats"))
            h_ready, parts_ready = sem("h_ready1"), sem("parts_ready1")
            gathered = sem("gathered1")
            half_added = sem("half_added1")
            taken = sem("taken1")

            with nc.Block() as block:
                @block.sync
                def _(sp):
                    for t in range(4):
                        fetch_tile(sp, t, slots[:, t], fetched[t])
                    with sp.Fori(1, NT // 4) as i:
                        for k in range(4):
                            sp.wait_ge(gathered, 4 * i + k - 3)
                            fetch_tile(sp, 4 * i + k, slots[:, k], fetched[k])

                @block.scalar
                def _(act):
                    take_root(act, squared_ready, root_ready, 1)
                    act.wait_ge(squared_ready, 2)
                    nc.scalar.activation(root[:], deg[:], ACT.Sqrt).then_inc(root_ready, 1)
                    normalise(act, stats_ready, h, h_ready)

                @block.tensor
                def _(pe):
                    pe.wait_ge(parts_ready, NT)
                    with pe.Fori(0, NT // 4) as i:
                        for k in range(4):
                            pe.wait_ge(fetched[k], 16 * i + 16)
                            pe.wait_ge(taken, 4 * i + k + 1)
                            stand_alone(pe)
                            gather(slots[:, k], h_parts, ps_g[:, k % 2, :], range(NT)).then_inc(gathered, 1)

                @block.vector
                def _(dve):
                    dve.sem_inc(taken, 2)
                    link = chained(dve, steps)
                    norm_statistics(dve, link, moments, squared_ready, root_ready, 1)
                    dve.sem_inc(stats_ready, 1)
                    dve.sem_inc(squared_ready, 1)
                    dve.wait_ge(root_ready, 2)
                    link(nc.vector.tensor_scalar(tmp[:], root[:], NORM_EPS, None, ALU.max))
                    link(nc.vector.reciprocal(inv_norm[:], tmp[:]))
                    link(nc.vector.tensor_scalar(inc_scale[:], inv_norm[:], 1.0, None, ALU.add))
                    link(nc.vector.tensor_tensor(tmp[:], inc_scale[:], deg[:], ALU.mult))
                    link(nc.vector.reciprocal(row_scale[:], tmp[:]))
                    link(nc.vector.tensor_tensor(row_scale[:], row_scale[:], inc_scale[:], ALU.mult))
                    dve.wait_ge(h_ready, NT)
                    split_rows(dve, h_parts, parts_ready)
                    with dve.Fori(0, NT // 2) as i2:
                        for k in range(2):
                            t = 2 * i2 + k
                            rows = acc[:, bass.ds(t, 1), :].rearrange("p t d -> p (t d)")
                            scale = row_scale[:, bass.ds(t, 1)]
                            dve.wait_ge(gathered, t + 1)
                            nc.vector.scalar_tensor_tensor(out=rows, in0=ps_g[:, k, 0:D], scalar=scale,
                                                           in1=rows, op0=ALU.mult, op1=ALU.add)\
                                .then_inc(half_added, 1)
                            dve.wait_ge(half_added, t + 1)
                            nc.vector.scalar_tensor_tensor(out=rows, in0=ps_g[:, k, D:2 * D], scalar=scale,
                                                           in1=rows, op0=ALU.mult, op1=ALU.add).then_inc(taken, 1)

    if stop >= 3:
        with ExitStack() as ctx:
            sb, ps, sem = allocators(ctx)
            hT = sb("hT2", [P, DC, N], F32)
            eT = sb("eT", [P, DC, N], F32)
            support = sb("support", [P, NT, D], F32)
            weight_sb = sb("weight_sb", [P, DC, D], F32)
            edge_sb = sb("edge_sb", [P, DC, D], F32)
            bias_rows = sb("bias_rows", [P, D], F32)
            node_rows = sb("node_rows", [P, D], F32)
            logits = sb("logits", [P, NT], F32)
            node_max = sb("node_max", [P, 3], F32)
            node_sum = sb("node_sum", [P, 3], F32)
            node_att = sb("node_att", [P, NT], F32)
            has_edge = sb("has_edge", [P, NT], F32)
            e_tile = sb("e_tile", [P, 2, DC, P], F32)
            mask = sb("mask2", [P, 2, N], BF16)
            mask_diag = sb("mask_diag2", [P, NT, P], BF16)
            probs = sb("probs2", [P, 2, N], F32)
            probs_t = sb("probs_t2", [P, 2, NT, P], F32)
            products = probs[:].rearrange("p k (t d) -> p (k t) d", d=D)
            row_max = sb("row_max2", [P, 2, 2], F32)
            neg_max = sb("neg_max2", [P, 2], F32)
            den = sb("den2", [P, 2], F32)
            rden = sb("rden2", [P, 2], F32)
            ps_s = ps("ps_s2", [P, 2, HALF])
            ps_ta = ps("ps_ta2", [P, GRP * P])
            ps_td = ps("ps_td2", [P, GRP * P])
            ps_o = ps("ps_o2", [P, 2, 512])
            ps_rows = ps_o[:].rearrange("p b (c q) -> p b c q", c=DC)

            w_in = sem("w_in2")
            steps, squared_ready, root_ready, stats_ready = (sem(f"{s}_2") for s in ("steps", "sq", "root", "stats"))
            h_ready, turned, evacuated = (sem(f"{s}_2") for s in ("h_ready", "turned", "evacuated"))
            proj_full = sem("proj_full2")
            proj_free = sem("proj_free2")
            max_ready, all_max, neg_ready = sem("max_ready"), sem("all_max"), sem("neg_ready")
            node_exp, all_sum = sem("node_exp"), sem("all_sum")
            mask_in = [sem(f"mask_in2{k}") for k in range(2)]
            mask_patched = sem("mask_patched")
            tile_ready = sem("tile_ready2")
            half_full = sem("half_full2")
            half_free = sem("half_free2")
            masked = sem("masked2")
            exped = sem("exped2")
            ta_full, ta_free = sem("ta_full2"), sem("ta_free2")
            td_full, td_free = sem("td_full2"), sem("td_free2")
            pv_done = sem("pv_done2")
            scale_steps = sem("scale_steps2")
            added = sem("added2")
            NPROJ = 4 + 4

            def each_tile(eng, body):
                with eng.Fori(0, NT // 2 - 1) as i:
                    body(2 * i, 0, True)
                    body(2 * i + 1, 1, True)
                body(NT - 2, 0, True)
                body(NT - 1, 1, False)

            with nc.Block() as block:
                @block.sync
                def _(sp):
                    sp.dma_start(edge_sb[:], edge_w.rearrange("(c p) o -> p c o", p=P)).then_inc(w_in, 16)
                    sp.dma_start(weight_sb[:], weight.rearrange("(c p) o -> p c o", p=P)).then_inc(w_in, 16)
                    sp.dma_start(node_rows[:], node_w.rearrange("d a -> (d a)").partition_broadcast(P))\
                        .then_inc(w_in, 16)
                    sp.dma_start(bias_rows[:], bias.partition_broadcast(P)).then_inc(w_in, 16)
                    sp.dma_start(mask_diag[:], diag_dram).then_inc(w_in, 16)
                    with sp.Fori(0, NT // 2) as i2:
                        for k in range(2):
                            sp.wait_ge(masked, 2 * i2 + k + 1)
                            sp.dma_start(mask[:, k, :], mask_dram[2 * i2 + k]).then_inc(mask_in[k], 16)

                @block.gpsimd
                def _(pool):
                    pool.wait_ge(max_ready, 1)
                    nc.gpsimd.partition_all_reduce(node_max[:, 1:2], node_max[:, 0:1], P, RMAX).then_inc(all_max, 1)
                    pool.wait_ge(node_exp, 1)
                    nc.gpsimd.partition_all_reduce(node_sum[:, 1:2], node_sum[:, 0:1], P, RADD).then_inc(all_sum, 1)
                    pool.wait_ge(proj_free, 2 + 4)
                    with pool.Fori(0, NT // 2) as i2:
                        for k in range(2):
                            t = 2 * i2 + k
                            pool.wait_ge(half_full, 2 * t + 2)
                            nc.gpsimd.tensor_copy(e_tile[:, k], eT[:, :, bass.ds(t * P, P)])\
                                .then_inc(tile_ready, 1)

                @block.tensor
                def _(pe):
                    pe.sem_inc(half_full, 4)
                    pe.sem_inc(td_full, 4)
                    pe.sem_inc(pv_done, 2)
                    turn_rows(pe, h, h_ready, ps_rows, turned, evacuated)
                    pe.wait_ge(evacuated, NT // 2)
                    pe.wait_ge(w_in, 5 * 16)
                    for n in range(4):
                        oc, half = n // 2, n % 2
                        pe.wait_ge(proj_free, n + 1)
                        for c in range(2):
                            first = half * HALF + c * 512
                            for dc in range(DC):
                                last = nc.tensor.matmul(ps_s[:, half, c * 512:(c + 1) * 512],
                                                        edge_sb[:, dc, oc * P:(oc + 1) * P],
                                                        hT[:, dc, first:first + 512],
                                                        start=(dc == 0), stop=(dc == DC - 1))
                        last.then_inc(proj_full, 1)
                    for n in range(4):
                        pe.wait_ge(proj_free, 4 + n + 1)
                        for t in range(4):
                            first = (4 * n + t) * P
                            for dc in range(DC):
                                last = nc.tensor.matmul(ps_s[:, n % 2, t * D:(t + 1) * D],
                                                        hT[:, dc, first:first + P], weight_sb[:, dc, :],
                                                        start=(dc == 0), stop=(dc == DC - 1))
                        last.then_inc(proj_full, 1)
                    pe.wait_ge(proj_free, NPROJ + 2)

                    def scores(t, k, half):
                        pe.wait_ge(tile_ready, t + 1)
                        pe.wait_ge(half_free, 2 * t + half + 1)
                        for c in range(2):
                            first = half * HALF + c * 512
                            for dc in range(DC):
                                last = nc.tensor.matmul(ps_s[:, half, c * 512:(c + 1) * 512], e_tile[:, k, dc, :],
                                                        eT[:, dc, first:first + 512],
                                                        start=(dc == 0), stop=(dc == DC - 1))
                        last.then_inc(half_full, 1)

                    def turn(t, k, grp):
                        bank, free, full = ((ps_ta, ta_free, ta_full), (ps_td, td_free, td_full))[grp % 2]
                        pe.wait_ge(free, 2 * t + grp // 2 + 1)
                        for n in range(GRP):
                            j = GRP * grp + n
                            last = nc.tensor.transpose(bank[:, n * P:(n + 1) * P], probs[:, k, j * P:(j + 1) * P],
                                                       ident[:])
                        last.then_inc(full, 1)

                    for half in range(2):
                        scores(0, 0, half)

                    def tile_body(t, k, more):
                        if more:
                            scores(t + 1, 1 - k, 0)
                        pe.wait_ge(exped, t + 1)
                        turn(t, k, 0)
                        turn(t, k, 1)
                        if more:
                            scores(t + 1, 1 - k, 1)
                        turn(t, k, 2)
                        turn(t, k, 3)
                        pe.wait_ge(added, t + 1)
                        pe.wait_ge(ta_free, 2 * t + 3)
                        pe.wait_ge(td_free, 2 * t + 3)
                        for j in range(NT):
                            last = nc.tensor.matmul(ps_o[:, k, 0:D], probs_t[:, k, j, :], support[:, j, :],
                                                    start=(j == 0), stop=(j == NT - 1))
                        last.then_inc(pv_done, 1)

                    each_tile(pe, tile_body)

                @block.scalar
                def _(act):
                    act.sem_inc(proj_free, 2)
                    act.sem_inc(ta_free, 1)
                    take_root(act, squared_ready, root_ready, 1)
                    normalise(act, stats_ready, h, h_ready)
                    for n in range(4):
                        oc, half = n // 2, n % 2
                        act.wait_ge(proj_full, n + 1)
                        nc.scalar.activation(eT[:, oc, half * HALF:(half + 1) * HALF], ps_s[:, half, :], ACT.Copy)\
                            .then_inc(proj_free, 1)
                    for n in range(4):
                        act.wait_ge(proj_full, 4 + n + 1)
                        nc.scalar.activation(support[:, 4 * n:4 * n + 4, :],
                                             ps_s[:, n % 2, :].rearrange("p (t d) -> p t d", d=D), ACT.Copy)\
                            .then_inc(proj_free, 1)
                    act.wait_ge(neg_ready, 1)
                    nc.scalar.activation(node_att[:], logits[:], ACT.Exp, bias=node_max[:, 2:3],
                                         accum_out=node_sum[:, 0:1]).then_inc(node_exp, 1)

                    def exponentials(t, k):
                        act.wait_ge(masked, t + 3)
                        nc.scalar.activation(probs[:, k, :], probs[:, k, :], ACT.Exp, bias=neg_max[:, k:k + 1],
                                             accum_out=den[:, k:k + 1]).then_inc(exped, 1)

                    exponentials(0, 0)

                    def tile_body(t, k, more):
                        act.wait_ge(pv_done, t + 1)
                        for n in range(2):
                            act.wait_ge(ta_full, 2 * t + n + 1)
                            nc.scalar.activation(probs_t[:, k, 2 * GRP * n:2 * GRP * n + GRP, :],
                                                 ps_ta[:].rearrange("p (j q) -> p j q", q=P), ACT.Copy)\
                                .then_inc(ta_free, 1)
                        if more:
                            exponentials(t + 1, 1 - k)

                    each_tile(act, tile_body)

                @block.vector
                def _(dve):
                    dve.sem_inc(half_free, 2)
                    dve.sem_inc(masked, 2)
                    dve.sem_inc(td_free, 1)
                    dve.sem_inc(added, 2)
                    link = chained(dve, steps)
                    norm_statistics(dve, link, moments, squared_ready, root_ready, 1)
                    dve.sem_inc(stats_ready, 1)
                    store_turned(dve, hT, ps_rows, turned, evacuated)
                    dve.wait_ge(w_in, 5 * 16)
                    for t in range(NT):
                        last = nc.vector.tensor_tensor_reduce(products[:, t, :], h[:, t, :], node_rows[:], 1.0, 0.0,
                                                              ALU.mult, ALU.add, logits[:, t:t + 1])
                    link(last)
                    nc.vector.tensor_reduce(node_max[:, 0:1], logits[:], AX_X, ALU.max).then_inc(max_ready, 1)
                    dve.wait_ge(all_max, 1)
                    nc.vector.tensor_scalar(node_max[:, 2:3], node_max[:, 1:2], -1.0, None, ALU.mult)\
                        .then_inc(neg_ready, 1)
                    link(nc.vector.tensor_tensor(acc[:], acc[:], bias_rows[:].unsqueeze(1).to_broadcast([P, NT, D]),
                                                 ALU.add))
                    link(nc.vector.tensor_scalar(has_edge[:], deg[:], 1.0, None, ALU.min))
                    dve.wait_ge(all_sum, 1)
                    link(nc.vector.reciprocal(node_sum[:, 2:3], node_sum[:, 1:2]))
                    link(nc.vector.scalar_tensor_tensor(out=node_att[:], in0=node_att[:], scalar=node_sum[:, 2:3],
                                                        in1=has_edge[:], op0=ALU.mult, op1=ALU.mult))

                    def mask_half(t, k, half):
                        if half == 0:
                            dve.wait_ge(mask_in[k], 8 * t - 8 * k + 16)
                            nc.vector.tensor_copy(mask[:, k, bass.ds(t * P, P)],
                                                  mask_diag[:, bass.ds(t, 1), :].rearrange("p t q -> p (t q)"))\
                                .then_inc(mask_patched, 1)
                            dve.wait_ge(mask_patched, t + 1)
                            dve.wait_ge(td_full, 2 * t + 2)
                        dve.wait_ge(half_full, 2 * t + half + 5)
                        stand_alone(dve)
                        nc.vector.tensor_tensor_reduce(
                            probs[:, k, half * HALF:(half + 1) * HALF], ps_s[:, half, :],
                            mask[:, k, half * HALF:(half + 1) * HALF], 1.0, LOWEST, ALU.add, ALU.max,
                            row_max[:, k, half:half + 1]).then_inc(half_free, 1)

                    def finish_mask(t, k):
                        dve.wait_ge(half_free, 2 * t + 4)
                        nc.vector.tensor_reduce(neg_max[:, k:k + 1], row_max[:, k, :], AX_X, ALU.max, negate=True)\
                            .then_inc(masked, 1)

                    def copy_group(t, k, n):
                        dve.wait_ge(td_full, 2 * t + n + 5)
                        nc.vector.tensor_copy(probs_t[:, k, GRP + 2 * GRP * n:2 * GRP + 2 * GRP * n, :],
                                              ps_td[:].rearrange("p (j q) -> p j q", q=P)).then_inc(td_free, 1)

                    mask_half(0, 0, 0)
                    mask_half(0, 0, 1)
                    finish_mask(0, 0)

                    def tile_body(t, k, more):
                        dve.wait_ge(pv_done, t + 1)
                        if more:
                            mask_half(t + 1, 1 - k, 0)
                        copy_group(t, k, 0)
                        if more:
                            mask_half(t + 1, 1 - k, 1)
                            finish_mask(t + 1, 1 - k)
                        copy_group(t, k, 1)
                        nc.vector.reciprocal(rden[:, k:k + 1], den[:, k:k + 1]).then_inc(scale_steps, 1)
                        dve.wait_ge(scale_steps, 2 * t + 1)
                        scale = row_scale[:, bass.ds(t, 1)]
                        nc.vector.tensor_tensor(scale, rden[:, k:k + 1], node_att[:, bass.ds(t, 1)], ALU.mult)\
                            .then_inc(scale_steps, 1)
                        dve.wait_ge(scale_steps, 2 * t + 2)
                        dve.wait_ge(pv_done, t + 3)
                        rows = acc[:, bass.ds(t, 1), :].rearrange("p t d -> p (t d)")
                        nc.vector.scalar_tensor_tensor(out=rows, in0=ps_o[:, k, 0:D], scalar=scale, in1=rows,
                                                       op0=ALU.mult, op1=ALU.add).then_inc(added, 1)

                    each_tile(dve, tile_body)

    if stop >= 4:
        with ExitStack() as ctx:
            sb, ps, sem = allocators(ctx)
            w3_sb = sb("w3_sb", [P, DC, D], F32)
            w3_t = sb("w3_t", [P, DC, D], F32)
            b3_rows = sb("b3_rows", [P, D], F32)
            d_root = sb("d_root", [P, NT], F32)
            with_self = sb("with_self", [P, 2, D], F32)
            z = sb("z", [P, 2, D], F32)
            z_t = sb("z_t", [P, 2, DC, P], F32)
            linear = sb("linear", [P, 2, D], F32)
            h_parts = sb("h_parts3", [P, NT, 2, D], F16)
            slots = sb("slots3", [P, 2, NT, P], F8)
            ps_g = ps("ps_g3", [P, 2, 2 * D])
            fetched = [sem(f"fetched3{k}") for k in range(2)]
            ps_z = ps("ps_z", [P, 2, 512])
            ps_f = ps("ps_f", [P, 2, 512])

            w_in = sem("w_in3")
            steps, squared_ready, root_ready, stats_ready = (sem(f"{s}_3") for s in ("steps", "sq", "root", "stats"))
            h_ready, parts_ready = sem("h_ready3"), sem("parts_ready3")
            w3_turned, w3_ready = sem("w3_turned"), sem("w3_ready")
            gathered, z_steps, z_ready = sem("gathered3"), sem("z_steps"), sem("z_ready")
            z_turned, z_t_ready = sem("z_turned"), sem("z_t_ready")
            final_ready, linear_ready, rows_ready = sem("final_ready"), sem("linear_ready"), sem("rows_ready")
            stored = sem("stored")

            def each_round(eng, body):
                body(0, 0, False, False)
                with eng.Fori(0, NT // 2 - 1) as i:
                    body(2 * i + 1, 1, True, False)
                    body(2 * i + 2, 0, True, False)
                body(NT - 1, 1, True, False)
                body(NT, 0, True, True)

            with nc.Block() as block:
                @block.sync
                def _(sp):
                    sp.dma_start(w3_sb[:], W3.rearrange("(c p) i -> p c i", p=P)).then_inc(w_in, 16)
                    sp.dma_start(b3_rows[:], b3.partition_broadcast(P)).then_inc(w_in, 16)
                    with sp.Fori(0, NT) as t:
                        sp.wait_ge(rows_ready, t + 1)
                        sp.dma_start(out[bass.ds(t * P, P), :],
                                     acc[:, bass.ds(t, 1), :].rearrange("p t d -> p (t d)")).then_inc(stored, 16)
                    sp.wait_ge(stored, 16 * NT)

                @block.gpsimd
                def _(pool):
                    for t in range(2):
                        fetch_tile(pool, t, slots[:, t], fetched[t])
                    with pool.Fori(1, NT // 2) as i:
                        for k in range(2):
                            pool.wait_ge(gathered, 2 * i + k - 1)
                            stand_alone(pool)
                            fetch_tile(pool, 2 * i + k, slots[:, k], fetched[k])

                @block.tensor
                def _(pe):
                    pe.wait_ge(w_in, 2 * 16)
                    for ic in range(DC):
                        for oc in range(DC):
                            last = nc.tensor.transpose(ps_z[:, ic, oc * P:(oc + 1) * P],
                                                       w3_sb[:, oc, ic * P:(ic + 1) * P], ident[:])
                    last.then_inc(w3_turned, 1)
                    pe.wait_ge(w3_ready, 1)
                    pe.wait_ge(parts_ready, NT)

                    def round_body(t, k, previous, only):
                        if not only:
                            pe.wait_ge(fetched[k], 8 * (t - k) + 16)
                            stand_alone(pe)
                            gather(slots[:, k], h_parts, ps_g[:, k, :], range(NT // 2))
                        if previous:
                            pe.wait_ge(z_ready, t)
                            for dc in range(DC):
                                last = nc.tensor.transpose(ps_z[:, 1 - k, dc * P:(dc + 1) * P],
                                                           z[:, 1 - k, dc * P:(dc + 1) * P], ident[:])
                            last.then_inc(z_turned, 1)
                        if not only:
                            gather(slots[:, k], h_parts, ps_g[:, k, :], range(NT // 2, NT)).then_inc(gathered, 1)
                        if previous:
                            pe.wait_ge(z_t_ready, t)
                            for dc in range(DC):
                                last = nc.tensor.matmul(ps_f[:, 1 - k, 0:D], z_t[:, 1 - k, dc, :], w3_t[:, dc, :],
                                                        start=(dc == 0), stop=(dc == DC - 1))
                            last.then_inc(final_ready, 1)

                    each_round(pe, round_body)

                @block.scalar
                def _(act):
                    take_root(act, squared_ready, root_ready, 1)
                    take_root(act, squared_ready, root_ready, 2)
                    act.wait_ge(w3_turned, 1)
                    nc.scalar.activation(w3_t[:], ps_z[:, :, 0:D], ACT.Copy).then_inc(w3_ready, 1)
                    normalise(act, stats_ready, h, h_ready)

                    def round_body(t, k, previous, only):
                        if previous:
                            act.wait_ge(z_turned, t)
                            nc.scalar.activation(z_t[:, 1 - k], ps_z[:, 1 - k, 0:D]
                                                 .rearrange("p (c q) -> p c q", c=DC), ACT.Copy).then_inc(z_t_ready, 1)

                    each_round(act, round_body)

                @block.vector
                def _(dve):
                    link = chained(dve, steps)
                    link(nc.vector.tensor_scalar(squared[:], deg[:], 1.0, None, ALU.add))
                    inverse_root(dve, link, squared_ready, root_ready, 1)
                    link(nc.vector.tensor_copy(d_root[:], rstd[:]))
                    norm_statistics(dve, link, moments, squared_ready, root_ready, 2)
                    link(nc.vector.tensor_tensor(rstd[:], rstd[:], d_root[:], ALU.mult))
                    nc.vector.tensor_tensor(nbias[:], nbias[:], d_root[:], ALU.mult).then_inc(stats_ready, 1)
                    dve.wait_ge(h_ready, NT)
                    split_rows(dve, h_parts, parts_ready)
                    dve.wait_ge(w_in, 2 * 16)

                    def round_body(t, k, previous, only):
                        if not only:
                            dve.wait_ge(gathered, t + 1)
                            nc.vector.tensor_tensor(with_self[:, k, :], ps_g[:, k, 0:D],
                                                    h[:, bass.ds(t, 1), :].rearrange("p t d -> p (t d)"), ALU.add)\
                                .then_inc(z_steps, 1)
                            dve.wait_ge(z_steps, t + 1)
                            nc.vector.tensor_tensor(z[:, k, :], ps_g[:, k, D:2 * D], with_self[:, k, :], ALU.add)\
                                .then_inc(z_ready, 1)
                        if previous:
                            dve.wait_ge(final_ready, t)
                            rows = acc[:, bass.ds(t - 1, 1), :].rearrange("p t d -> p (t d)")
                            nc.vector.scalar_tensor_tensor(out=linear[:, 1 - k, :], in0=ps_f[:, 1 - k, 0:D],
                                                           scalar=d_root[:, bass.ds(t - 1, 1)], in1=b3_rows[:],
                                                           op0=ALU.mult, op1=ALU.add).then_inc(linear_ready, 1)
                            dve.wait_ge(linear_ready, t)
                            nc.vector.scalar_tensor_tensor(out=rows, in0=linear[:, 1 - k, :], scalar=0.0, in1=rows,
                                                           op0=ALU.max, op1=ALU.add).then_inc(rows_ready, 1)

                    each_round(dve, round_body)
    else:
        with ExitStack() as ctx:
            _, _, sem = allocators(ctx)
            stored = sem("stored")
            with nc.Block() as block:
                @block.sync
                def _(sp):
                    sp.dma_start(out.rearrange("(t p) d -> p t d", p=P), acc[:]).then_inc(stored, 16)
                    sp.wait_ge(stored, 16)
    late.close()
    whole.close()


_INS = ['x', 'adj', 'L0_gnn_Wks', 'L0_gnn_Wqs', 'L0_gnn_Wvs', 'L0_gnn_Wo', 'L2_gnn_weight', 'L2_gnn_bias',
        'L2_gnn_node_w', 'L2_gnn_edge_w', 'L3_gnn_W', 'L3_gnn_b']


def kernel(**inputs):
    import numpy as _np
    import concourse.bacc as _bacc
    from concourse import mybir as _mybir
    from concourse.bass_utils import run_bass_kernel_spmd as _run

    nc = _bacc.Bacc("TRN2", target_bir_lowering=False, num_devices=1)
    arrays, args = {}, []
    for name in _INS:
        a = _np.ascontiguousarray(inputs[name])
        arrays[f"in_{name}_dram"] = a
        args.append(nc.dram_tensor(f"in_{name}_dram", a.shape, _mybir.dt.from_np(a.dtype), kind="ExternalInput").ap())
    args.append(nc.dram_tensor("out_dram", (N, D), F32, kind="ExternalOutput").ap())
    program(nc, *args)
    r = _run(nc, [arrays], core_ids=[0])
    return r.results[0]["out_dram"]
```

```python
from contextlib import ExitStack

import concourse.bass as bass
from concourse import mybir

F32 = mybir.dt.float32
F16 = mybir.dt.float16
BF16 = mybir.dt.bfloat16
F8 = mybir.dt.float8e4
U16 = mybir.dt.uint16
ALU = mybir.AluOpType
ACT = mybir.ActivationFunctionType
AX_X = mybir.AxisListType.X
RMAX = bass.bass_isa.ReduceOp.max
RADD = bass.bass_isa.ReduceOp.add

P = 128
N = 2048
D = 256
NT = N // P
DC = D // P
H = 8
KD = 64
PAIRS = H // 2
NCH = NT // 2
CQ = 2 * P
UPC = 4
UPP = NCH * UPC
HALF = N // 2
AHEAD = 2
HPP = 6 + 2 * UPP
K_HALF, V_HALF = 2, 8
GRP = 4
VECTOR_GROUP = 3
BIG = 2.0 ** 53
IDENTITY_BIAS = 0.01
LN_EPS = 1e-5
NORM_EPS = 1e-12
LOWEST = -3.0e38
ALL, FIRST, LAST = slice(0, NT), slice(0, NT - 2), slice(NT - 2, NT)



def program(nc, x, adj, Wks, Wqs, Wvs, Wo, weight, bias, node_w, edge_w, W3, b3, out):
    mask_dram = nc.dram_tensor("mask_rows", (NT, P, N), BF16).ap()

    def allocators(ctx):
        def sb(name, shape, dt):
            return ctx.enter_context(nc.sbuf_tensor(name, shape, dt))

        def ps(name, shape, dt=F32):
            return ctx.enter_context(nc.psum_tensor(name, shape, dt))

        def sem(name):
            return ctx.enter_context(nc.semaphore(name))
        return sb, ps, sem

    whole = ExitStack()
    sb, _, _ = allocators(whole)
    acc = sb("acc", [P, NT, D], F32)
    ident = sb("ident", [P, P], F32)
    deg = sb("deg", [P, NT], F32)
    adjt = sb("adjt", [P, NT, NT, P], F8)
    stats = sb("stats", [P, NT, 6], F32)
    meanvar = sb("meanvar", [P, NT, 2], F32)
    squared = sb("squared", [P, NT], F32)
    root = sb("root", [P, NT], F32)
    tmp = sb("tmp", [P, NT], F32)
    rstd = sb("rstd", [P, NT], F32)
    nbias = sb("nbias", [P, NT], F32)

    def stand_alone(eng):
        eng.nop(nofuse=True)

    def chained(eng, sem):
        count = [0]

        def link(ins):
            count[0] += 1
            ins.then_inc(sem, 1)
            eng.wait_ge(sem, count[0])
        return link

    def inverse_root(dve, link, tiles, result, squared_ready, root_ready, n):
        dve.sem_inc(squared_ready, 1)
        dve.wait_ge(root_ready, n)
        y, t, v = result[:, tiles], tmp[:, tiles], squared[:, tiles]
        link(nc.vector.reciprocal(y, root[:, tiles]))
        link(nc.vector.tensor_tensor(t, y, y, ALU.mult))
        link(nc.vector.tensor_tensor(t, t, v, ALU.mult))
        link(nc.vector.tensor_scalar(t, t, -0.5, 1.5, ALU.mult, ALU.add))
        link(nc.vector.tensor_tensor(y, y, t, ALU.mult))

    def take_stats(t):
        return nc.vector.bn_stats(stats[:, bass.ds(t, 1), :].rearrange("p t s -> p (t s)"),
                                  acc[:, bass.ds(t, 1), :].rearrange("p t d -> p (t d)"))

    def norm_factors(dve, link, tiles, squared_ready, root_ready, n, scale=None):
        for t in range(tiles.start, tiles.stop):
            last = nc.vector.bn_aggr(meanvar[:, t, :], stats[:, t, :])
        link(last)
        link(nc.vector.tensor_scalar(squared[:, tiles], meanvar[:, tiles, 1], LN_EPS, None, ALU.add))
        inverse_root(dve, link, tiles, rstd, squared_ready, root_ready, n)
        if scale is not None:
            link(nc.vector.tensor_tensor(rstd[:, tiles], rstd[:, tiles], scale[:, tiles], ALU.mult))
        link(nc.vector.scalar_tensor_tensor(out=nbias[:, tiles], in0=meanvar[:, tiles, 0], scalar=-1.0,
                                            in1=rstd[:, tiles], op0=ALU.mult, op1=ALU.mult))

    def take_root(act, tiles, squared_ready, root_ready, n):
        act.wait_ge(squared_ready, n)
        nc.scalar.activation(root[:, tiles], squared[:, tiles], ACT.Sqrt).then_inc(root_ready, 1)

    def normalise(act, squared_ready, root_ready, stats_ready, h, h_ready, tiles):
        for t in range(NT):
            if t == min(2, tiles.start):
                take_root(act, tiles, squared_ready, root_ready, 1)
            if t == tiles.start:
                act.wait_ge(stats_ready, 1)
            nc.scalar.activation(h[:, t, :], acc[:, t, :], ACT.Relu, bias=nbias[:, t:t + 1],
                                 scale=rstd[:, t:t + 1]).then_inc(h_ready, 1)

    def turn_rows(pe, h, h_ready, ps_rows, turned, evacuated):
        for g in range(NT // 2):
            pe.wait_ge(h_ready, 2 * g + 2)
            if g >= 2:
                pe.wait_ge(evacuated, g - 1)
            for dc in range(DC):
                for k in range(2):
                    last = nc.tensor.transpose(ps_rows[:, g % 2, dc, k * P:(k + 1) * P],
                                               h[:, 2 * g + k, dc * P:(dc + 1) * P], ident[:])
            last.then_inc(turned, 1)

    def store_turned(dve, hT, ps_rows, turned, evacuated):
        for g in range(NT // 2):
            dve.wait_ge(turned, g + 1)
            nc.vector.tensor_copy(hT[:, :, g * 2 * P:(g + 1) * 2 * P], ps_rows[:, g % 2])\
                .then_inc(evacuated, 1)

    layer0 = ExitStack()
    sb0, ps0, sem0 = allocators(layer0)
    hT = sb0("hT", [P, DC, N], F32)
    w_pair = sb0("w_pair", [P, 3, DC, 2 * KD], F32)
    q_parts = sb0("q_parts", [P, 2, N], F16)
    k_parts = sb0("k_parts", [P, 2, 2, N], F16)
    mask = sb0("mask", [P, 2, N], BF16)
    not_eye = sb0("not_eye", [P, P], BF16)
    probs = sb0("probs", [P, UPC, N], F32)
    probs_t = sb0("probs_t", [P, 2, 2, NT, CQ], F32)
    STAGED = 8
    staged = probs_t[:, 1].rearrange("p a j q -> p (a j q)").bitcast(BF16).rearrange("p (t n) -> p t n", n=N)
    ps_s = ps0("ps_s", [P, 2, HALF])

    w_in = sem0("w_in")
    half_full = sem0("half_full")
    half_free = sem0("half_free")
    hi_ready = sem0("hi_ready")
    k_doubled = [sem0(f"k_doubled{half}") for half in range(2)]
    mask_out = [sem0(f"mask_out{k}") for k in range(2)]

    def load_pair(pool, pair):
        for n, w in enumerate((Wqs, Wks, Wvs)):
            for a in range(2):
                pool.dma_start(w_pair[:, n, :, a * KD:(a + 1) * KD],
                               w[bass.ds(2 * pair + a, 1)].rearrange("h (c p) k -> p (h c) k", p=P))\
                    .then_inc(w_in, 16)

    def free_half(pe, pair, n):
        pe.wait_ge(half_free, HPP * pair + n + 1)

    def project(pe, pair, n, half):
        if half == 0 and n == 0:
            pe.wait_ge(w_in, 6 * 16 * (pair + 1))
        free_half(pe, pair, 2 * n + half)
        for c in range(2):
            for dc in range(DC):
                first = half * HALF + c * 512
                last = nc.tensor.matmul(ps_s[:, half, c * 512:(c + 1) * 512], w_pair[:, n, dc, :],
                                        hT[:, dc, first:first + 512], start=(dc == 0), stop=(dc == DC - 1))
        last.then_inc(half_full, 1)

    def hi_parts(act, pair, n, half):
        act.wait_ge(half_full, HPP * pair + 2 * n + half + 1)
        cols = slice(half * HALF, (half + 1) * HALF)
        for a in range(2):
            hi = (q_parts[0:KD, a, cols], k_parts[0:KD, a, 0, cols])[n]
            last = nc.scalar.activation(hi, ps_s[a * KD:(a + 1) * KD, half, :], ACT.Copy, scale=(KD ** -0.5, 1.0)[n])
        last.then_inc(hi_ready, 1)

    def lo_parts(dve, pair, n, half):
        dve.wait_ge(hi_ready, 4 * pair + 2 * n + half + 1)
        cols = slice(half * HALF, (half + 1) * HALF)
        for a in range(2):
            if n == 0:
                hi, lo = q_parts[0:KD, a, cols], q_parts[KD:P, a, cols]
            else:
                hi, lo = k_parts[0:KD, a, 0, cols], k_parts[0:KD, a, 1, cols]
            last = nc.vector.scalar_tensor_tensor(out=lo, in0=ps_s[a * KD:(a + 1) * KD, half, :],
                                                  scalar=(KD ** -0.5, 1.0)[n], in1=hi,
                                                  op0=ALU.mult, op1=ALU.subtract)
        last.then_inc(half_free, 1)

    def double_k(sp, pair):
        for half in range(2):
            sp.wait_ge(half_free, HPP * pair + K_HALF + half + 3)
            cols = slice(half * HALF, (half + 1) * HALF)
            sp.dma_start(k_parts[KD:P, :, :, cols], k_parts[0:KD, :, :, cols]).then_inc(k_doubled[half], 16)

    with ExitStack() as ctx:
        sb, ps, sem = allocators(ctx)
        h = probs[:, 0:2, :].rearrange("p a (t d) -> p (a t) d", d=D)
        adj16 = probs[:, 2, :].bitcast(F16).rearrange("p (k n) -> p k n", n=N)
        adj_in = probs_t[:, 0].rearrange("p a (b j) q -> p (a b) (j q)", b=2)
        ident16 = sb("ident16", [P, P], F16)
        ps_adjt = ps("ps_adjt", [P, 2, N], F16)
        ps_rows = ps_s[:, :, 0:512].rearrange("p b (c q) -> p b c q", c=DC)

        x_in = sem("x_in")
        adj_loaded = [sem(f"adj_loaded{k}") for k in range(4)]
        filled, consts = sem("consts_filled"), sem("consts_ready")
        steps, squared_ready, root_ready, stats_ready = (sem(f"{s}_in") for s in ("steps", "sq", "root", "stats"))
        h_ready, turned, evacuated = (sem(f"{s}_in") for s in ("h_ready", "turned", "evacuated"))
        adj_copied = sem("adj_copied")
        masked = sem("masked_in")
        adj_turned = sem("adj_turned")
        adjt_stored = sem("adjt_stored")

        def interleaved(eng, tile, norm, part, tile_first=False, unrolled=False):
            for t in range(2):
                tile(t, t)
            norm()
            for t in range(2, 4):
                tile(t, t)
            for n in range(2):
                for half in range(2):
                    if tile_first:
                        tile(4 + 2 * n + half, 2 * n + half)
                    part(n, half)
                    if not tile_first:
                        tile(4 + 2 * n + half, 2 * n + half)
            if unrolled:
                for t in range(8, NT):
                    tile(t, t % 4)
            else:
                with eng.Fori(2, NT // 4) as i:
                    for k in range(4):
                        tile(4 * i + k, k)

        with nc.Block() as block:
            @block.sync
            def _(sp):
                for k in range(2):
                    sp.sem_inc(mask_out[k], 16)

                def load(t, k):
                    sp.wait_ge(adj_copied, t + 1)
                    sp.dma_start(adj_in[:, k, :], adj[bass.ds(t * P, P), :]).then_inc(adj_loaded[k], 16)

                def store_mask(t, k):
                    sp.wait_ge(masked, t + 3)
                    sp.dma_start(mask_dram[t], mask[:, k, :]).then_inc(mask_out[k], 16)

                sp.dma_start(acc[:], x.rearrange("(t p) d -> p t d", p=P)).then_inc(x_in, 16)
                for t in range(4):
                    load(t, t)
                with sp.Fori(1, (NT - STAGED) // 4 + 1) as i:
                    for k in range(4):
                        load(4 * i + k, k)
                        store_mask(4 * i + k - 4, k % 2)
                for t in range(NT - STAGED + 4, NT):
                    load(t, t % 4)
                double_k(sp, 0)

            @block.gpsimd
            def _(pool):
                load_pair(pool, 0)
                nc.gpsimd.memset(ident[:], 0.0).then_inc(filled, 1)
                nc.gpsimd.memset(ident16[:], 0.0).then_inc(filled, 1)
                nc.gpsimd.memset(not_eye[:], 1.0).then_inc(filled, 1)
                pool.wait_ge(filled, 3)
                for m, v in ((ident, 1.0), (ident16, 1.0), (not_eye, 0.0)):
                    nc.gpsimd.affine_select(out=m[:], in_=m[:], compare_op=ALU.not_equal, fill=v, base=0,
                                            pattern=[[-1, P]], channel_multiplier=1).then_inc(consts, 1)
                pool.sem_inc(masked, 2)
                pool.wait_ge(consts, 3)

                def mask_tile(k, out):
                    nc.gpsimd.tensor_scalar(out, adj16[:, k, :], -1.0, BIG, ALU.add, ALU.mult).then_inc(masked, 1)

                with pool.Fori(0, (NT - STAGED) // 2) as i:
                    for k in range(2):
                        pool.wait_ge(adj_copied, 2 * i + k + 5)
                        pool.wait_ge(mask_out[k], 16 * i + 16)
                        stand_alone(pool)
                        mask_tile(k, mask[:, k, :])
                for n in range(STAGED):
                    pool.wait_ge(adj_copied, NT - STAGED + n + 5)
                    mask_tile(n % 2, staged[:, n, :])

            @block.scalar
            def _(act):
                act.sem_inc(adj_copied, 4)

                def copy_tile(t, slot):
                    k = slot % 2
                    act.wait_ge(adj_loaded[slot], 4 * (t - slot) + 16)
                    act.wait_ge(adj_turned, t + 1)
                    act.wait_ge(masked, t + 1)
                    nc.scalar.activation(adj16[:, k, :], adj_in[:, slot, :], ACT.Copy,
                                         accum_out=deg[:, bass.ds(t, 1)]).then_inc(adj_copied, 1)

                def norm():
                    normalise(act, squared_ready, root_ready, stats_ready, h, h_ready, ALL)

                interleaved(act, copy_tile, norm, lambda n, half: hi_parts(act, 0, n, half), tile_first=True)

            @block.tensor
            def _(pe):
                pe.sem_inc(adj_turned, 2)
                pe.wait_ge(consts, 3)

                def turn_tile(t, slot):
                    k = slot % 2
                    pe.wait_ge(adj_copied, t + 5)
                    pe.wait_ge(adjt_stored, t + 1)
                    for j in range(NT):
                        last = nc.tensor.transpose(ps_adjt[:, k, j * P:(j + 1) * P],
                                                   adj16[:, k, j * P:(j + 1) * P], ident16[:])
                    last.then_inc(adj_turned, 1)

                def norm():
                    turn_rows(pe, h, h_ready, ps_rows, turned, evacuated)
                    pe.wait_ge(evacuated, NT // 2)

                interleaved(pe, turn_tile, norm, lambda n, half: project(pe, 0, n, half))

            @block.vector
            def _(dve):
                dve.sem_inc(adjt_stored, 2)
                dve.sem_inc(half_free, 2)
                link = chained(dve, steps)
                dve.wait_ge(x_in, 16)
                for t in range(NT):
                    last = take_stats(t)
                link(last)
                norm_factors(dve, link, ALL, squared_ready, root_ready, 1)
                dve.sem_inc(stats_ready, 1)

                def store_tile(t, slot):
                    dve.wait_ge(adj_turned, t + 3)
                    nc.vector.tensor_copy(adjt[:, t].rearrange("p j q -> p (j q)"),
                                          ps_adjt[:, slot % 2, :], saturate=False).then_inc(adjt_stored, 1)

                interleaved(dve, store_tile, lambda: store_turned(dve, hT, ps_rows, turned, evacuated),
                            lambda n, half: lo_parts(dve, 0, n, half), unrolled=True)

    with ExitStack() as ctx:
        sb, ps, sem = allocators(ctx)
        wo_sb = sb("wo_sb", [P, D], F32)
        v_sb = sb("v_sb", [P, NT, 2 * KD], F32)
        row_max = sb("row_max", [P, UPC, 2], F32)
        neg_max = sb("neg_max", [P, UPC], F32)
        den = sb("den", [P, 2, UPC], F32)
        rden = sb("rden", [P, UPC], F32)
        rden_rows = sb("rden_rows", [P, UPC, KD], F32)
        o_normed = sb("o_normed", [P, CQ], F32)
        ps_t = ps("ps_t", [P, 2, GRP * P])
        ps_o = ps("ps_o", [P, 512])
        ps_x = ps("ps_x", [P, 512])

        wo_in = sem("wo_in")
        mask_in = [sem(f"mask_in{k}") for k in range(2)]
        staged_out = sem("staged_out")
        mask_patched = sem("mask_patched0")
        masked = sem("masked")
        exped = sem("exped")
        group_full = [sem(f"group_full{b}") for b in range(2)]
        group_free = [sem(f"group_free{b}") for b in range(2)]
        pv_done = sem("pv_done")
        rden_ready = sem("rden_ready")
        rden_turned = sem("rden_turned")
        rden_t_ready = sem("rden_t_ready")
        o_ready = sem("o_ready")
        out_ready = sem("out_ready")
        added = sem("added")
        stats_taken = sem("stats_taken")
        norm_steps, squared_ready, root_ready = (sem(f"{s}_tail0") for s in ("steps", "sq", "root"))
        steps = sem("steps0")

        def half_of(u, half):
            return (4 if isinstance(u, int) and u < AHEAD else 6) + 2 * u + half

        def each_chunk(eng, body):
            body(0, 0, True, False)
            with eng.Fori(0, (NCH - 2) // 2) as i:
                body(2 * i + 1, 1, False, False)
                body(2 * i + 2, 0, False, False)
            body(NCH - 1, 1, False, True)

        def each_pair(eng, body):
            with eng.Fori(0, PAIRS - 1) as pair:
                body(pair, False)
            body(PAIRS - 1, True)

        with nc.Block() as block:
            @block.sync
            def _(sp):
                def load_masks(pair, c, written=False):
                    for k in range(2):
                        if written:
                            sp.wait_ge(mask_out[k], 16 * (NT - STAGED) // 2 + 16)
                        sp.wait_ge(masked, UPP * pair + UPC * c + 2 * k + 2)
                        sp.dma_start(mask[:, k, :], mask_dram[2 * c + k]).then_inc(mask_in[k], 16)

                load_masks(0, 0, written=True)
                for n in range(STAGED):
                    sp.dma_start(mask_dram[NT - STAGED + n], staged[:, n, :]).then_inc(staged_out, 16)
                sp.wait_ge(staged_out, 16 * STAGED)
                with sp.Fori(1, NCH) as c:
                    load_masks(0, c)
                with sp.Fori(1, PAIRS) as pair:
                    load_masks(pair, 0)
                    double_k(sp, pair)
                    with sp.Fori(1, NCH) as c:
                        load_masks(pair, c)

            @block.gpsimd
            def _(pool):
                def load_wo(pair):
                    pool.dma_start(wo_sb[:], Wo[bass.ds(2 * pair, 2)].rearrange("a k o -> (a k) o"))\
                        .then_inc(wo_in, 16)

                load_wo(0)
                with pool.Fori(1, PAIRS) as pair:
                    pool.wait_ge(half_full, HPP * (pair - 1) + V_HALF + 2)
                    stand_alone(pool)
                    load_pair(pool, pair)
                    pool.wait_ge(out_ready, NCH * pair)
                    stand_alone(pool)
                    load_wo(pair)

            @block.tensor
            def _(pe):
                for b in range(2):
                    pe.sem_inc(group_full[b], 8)
                    pe.sem_inc(group_free[b], 1)
                pe.sem_inc(pv_done, 2)

                def project_v(pair, half):
                    free_half(pe, pair, V_HALF + half)
                    for t in range(NT // 2):
                        for dc in range(DC):
                            first = (half * NT // 2 + t) * P
                            last = nc.tensor.matmul(ps_s[:, half, t * P:(t + 1) * P],
                                                    hT[:, dc, first:first + P], w_pair[:, 2, dc, :],
                                                    start=(dc == 0), stop=(dc == DC - 1))
                    last.then_inc(half_full, 1)

                def scores(pair, u, q_tile, head, half):
                    free_half(pe, pair, half_of(u, half))
                    for n in range(2):
                        cols = slice(half * HALF + n * 512, half * HALF + (n + 1) * 512)
                        for part in range(2):
                            last = nc.tensor.matmul(ps_s[:, half, n * 512:(n + 1) * 512],
                                                    q_parts[:, head, bass.ds(q_tile * P, P)],
                                                    k_parts[:, head, part, cols],
                                                    start=(part == 0), stop=(part == 1))
                    last.then_inc(half_full, 1)

                def turn(g, w, grp):
                    pe.wait_ge(group_free[grp % 2], 2 * g + grp // 2 + 1)
                    for k in range(GRP):
                        j = GRP * grp + k
                        last = nc.tensor.transpose(ps_t[:, grp % 2, k * P:(k + 1) * P],
                                                   probs[:, w, j * P:(j + 1) * P], ident[:])
                    last.then_inc(group_full[grp % 2], 1)

                def attend(chunk, parity, js):
                    if js[0] == 0:
                        for b in range(2):
                            pe.wait_ge(group_free[b], 2 * UPC * (chunk + 1) + 1)
                        pe.wait_ge(o_ready, chunk + 1)
                    for j in js:
                        for a in range(2):
                            last = nc.tensor.matmul(ps_o[a * KD:(a + 1) * KD, 0:CQ],
                                                    v_sb[:, j, a * KD:(a + 1) * KD],
                                                    probs_t[:, parity, a, j, :],
                                                    start=(j == 0), stop=(j == NT - 1),
                                                    skip_group_check=True)
                    if js[-1] == NT - 1:
                        last.then_inc(pv_done, 1)

                def turn_rden(chunk):
                    pe.wait_ge(rden_ready, chunk + 1)
                    pe.wait_ge(added, chunk + 1)
                    for k in range(2):
                        last = nc.tensor.transpose(ps_x[:, k * P:(k + 1) * P],
                                                   rden_rows[:, 2 * k:2 * k + 2, :]
                                                   .rearrange("p a k -> p (a k)"), ident[:])
                    last.then_inc(rden_turned, 1)

                def project_out(chunk, pair):
                    pe.wait_ge(wo_in, 16 * (pair + 1))
                    pe.wait_ge(o_ready, chunk + 2)
                    for k in range(2):
                        last = nc.tensor.matmul(ps_x[:, k * D:(k + 1) * D], o_normed[:, k * P:(k + 1) * P],
                                                wo_sb[:], start=True, stop=True)
                    last.then_inc(out_ready, 1)

                def first_scores(pair):
                    for half in range(2):
                        pe.wait_ge(k_doubled[half], 16 * (pair + 1))
                        scores(pair, 0, 0, 0, half)

                def second_scores_and_v(pair):
                    for half in range(2):
                        scores(pair, 1, 0, 1, half)
                    for half in range(2):
                        project_v(pair, half)

                first_scores(0)
                second_scores_and_v(0)

                def pair_body(pair, last_pair):
                    def chunk_body(c, parity, first, last_chunk):
                        chunk = NCH * pair + c
                        for w in range(UPC):
                            g = UPC * chunk + w

                            def run_ahead(half):
                                if not last_chunk or w < UPC - AHEAD:
                                    scores(pair, UPC * c + w + AHEAD, 2 * c + (w + AHEAD) // 2, w % 2, half)
                                elif not last_pair:
                                    project(pe, pair + 1, w - (UPC - AHEAD), half)

                            run_ahead(0)
                            pe.wait_ge(exped, g + 1)
                            turn(g, w, 0)
                            turn(g, w, 1)
                            if w == 3 and not first:
                                attend(chunk - 1, 1 - parity, range(14, NT))
                            run_ahead(1)
                            turn(g, w, 2)
                            turn(g, w, 3)
                            if not first:
                                if w < 3:
                                    attend(chunk - 1, 1 - parity, (range(0, 5), range(5, 10), range(10, 14))[w])
                                if w == 1:
                                    turn_rden(chunk - 1)
                                if w == 3:
                                    project_out(chunk - 1, pair)

                    each_chunk(pe, chunk_body)
                    final = NCH * pair + NCH - 1
                    attend(final, 1, range(0, 10))
                    turn_rden(final)
                    attend(final, 1, range(10, NT))
                    if not last_pair:
                        first_scores(pair + 1)
                    project_out(final, pair)
                    if not last_pair:
                        second_scores_and_v(pair + 1)

                each_pair(pe, pair_body)

            @block.scalar
            def _(act):
                def exponentials(g, w, parity):
                    act.wait_ge(masked, g + UPC + 1)
                    nc.scalar.activation(probs[:, w, :], probs[:, w, :], ACT.Exp, bias=neg_max[:, w:w + 1],
                                         accum_out=den[:, parity, w:w + 1]).then_inc(exped, 1)

                def copy_group(g, w, parity, grp):
                    act.wait_ge(group_full[grp % 2], 2 * g + grp // 2 + 9)
                    first_j = GRP * grp
                    nc.scalar.activation(
                        probs_t[:, parity, w % 2, first_j:first_j + GRP, w // 2 * P:(w // 2 + 1) * P],
                        ps_t[:, grp % 2, :].rearrange("p (j q) -> p j q", q=P), ACT.Copy)\
                        .then_inc(group_free[grp % 2], 1)

                def copy_rden(chunk):
                    act.wait_ge(rden_turned, chunk + 1)
                    nc.scalar.activation(o_normed[:], ps_x[:, 0:CQ], ACT.Copy).then_inc(rden_t_ready, 1)

                for w in range(AHEAD):
                    exponentials(w, w, 0)

                def pair_body(pair, last_pair):
                    def chunk_body(c, parity, first, last_chunk):
                        chunk = NCH * pair + c
                        act.wait_ge(pv_done, chunk + 1)
                        for w in range(UPC):
                            g = UPC * chunk + w
                            ahead = not last_chunk or w < UPC - AHEAD
                            if w == 2 and not first:
                                copy_rden(chunk - 1)
                            for grp in range(GRP):
                                if grp != VECTOR_GROUP:
                                    copy_group(g, w, parity, grp)
                                if not ahead and not last_pair and grp % 2 == 1:
                                    hi_parts(act, pair + 1, w - (UPC - AHEAD), grp // 2)
                            if ahead:
                                exponentials(g + AHEAD, (w + AHEAD) % UPC, (parity + (w + AHEAD) // UPC) % 2)
                        if first:
                            act.wait_ge(staged_out, 16 * STAGED)

                    each_chunk(act, chunk_body)
                    if last_pair:
                        take_root(act, FIRST, squared_ready, root_ready, 1)
                    copy_rden(NCH * pair + NCH - 1)
                    if not last_pair:
                        for w in range(AHEAD):
                            exponentials(UPP * (pair + 1) + w, w, 0)

                each_pair(act, pair_body)

            @block.vector
            def _(dve):
                dve.sem_inc(masked, 4)
                dve.sem_inc(o_ready, 1)
                dve.sem_inc(added, 1)

                def copy_v(pair):
                    for half in range(2):
                        dve.wait_ge(half_full, HPP * pair + V_HALF + half + 1)
                        nc.vector.tensor_copy(v_sb[:, half * NT // 2:(half + 1) * NT // 2, :],
                                              ps_s[:, half, :].rearrange("p (t k) -> p t k", k=2 * KD))\
                            .then_inc(half_free, 1)

                def admit_diagonal(pair, q_tile, k):
                    dve.wait_ge(mask_in[k], 16 * NCH * pair + 8 * (q_tile - k) + 16)
                    diag = mask[:, k, bass.ds(q_tile * P, P)]
                    nc.vector.tensor_tensor(diag, diag, not_eye[:], ALU.mult).then_inc(mask_patched, 1)
                    dve.wait_ge(mask_patched, NT * pair + q_tile + 1)

                def mask_half(pair, u, w, half):
                    dve.wait_ge(half_full, HPP * pair + half_of(u, half) + 1)
                    if half == 0:
                        for b in range(2):
                            dve.wait_ge(group_full[b], 2 * (UPP * pair + u) + 2)
                    stand_alone(dve)
                    nc.vector.tensor_tensor_reduce(
                        probs[:, w, half * HALF:(half + 1) * HALF], ps_s[:, half, :],
                        mask[:, w // 2, half * HALF:(half + 1) * HALF], 1.0, LOWEST, ALU.add, ALU.max,
                        row_max[:, w, half:half + 1]).then_inc(half_free, 1)

                def finish_mask(pair, u, w, q_tile):
                    dve.wait_ge(half_free, HPP * pair + half_of(u, 1) + 3)
                    nc.vector.tensor_reduce(neg_max[:, w:w + 1], row_max[:, w, :], AX_X, ALU.max, negate=True)
                    diag = probs[:, w, bass.ds(q_tile * P, P)]
                    nc.vector.scalar_tensor_tensor(out=diag, in0=ident[:], scalar=IDENTITY_BIAS, in1=diag,
                                                   op0=ALU.mult, op1=ALU.add).then_inc(masked, 1)

                def mask_unit(pair, w):
                    if w == 0:
                        admit_diagonal(pair, 0, 0)
                    for half in range(2):
                        mask_half(pair, w, w, half)
                    finish_mask(pair, w, w, 0)

                def copy_group(g, w, parity, grp):
                    dve.wait_ge(group_full[grp % 2], 2 * g + grp // 2 + 9)
                    first_j = GRP * grp
                    nc.vector.tensor_copy(
                        probs_t[:, parity, w % 2, first_j:first_j + GRP, w // 2 * P:(w // 2 + 1) * P],
                        ps_t[:, grp % 2, :].rearrange("p (j q) -> p j q", q=P)).then_inc(group_free[grp % 2], 1)

                def spread_rden(chunk, parity):
                    nc.vector.reciprocal(rden[:], den[:, parity, :]).then_inc(steps, 1)
                    dve.wait_ge(steps, chunk + 1)
                    nc.vector.tensor_copy(rden_rows[:], rden[:].unsqueeze(2).to_broadcast([P, UPC, KD]))\
                        .then_inc(rden_ready, 1)

                def normalise_out(chunk):
                    dve.wait_ge(pv_done, chunk + 3)
                    dve.wait_ge(rden_t_ready, chunk + 1)
                    nc.vector.tensor_tensor(o_normed[:], ps_o[:, 0:CQ], o_normed[:], ALU.mult).then_inc(o_ready, 1)

                def add_out(chunk, c, last_pair):
                    dve.wait_ge(out_ready, chunk + 1)
                    rows = acc[:, bass.ds(2 * c, 2), :]
                    nc.vector.tensor_tensor(rows, ps_x[:].rearrange("p (t d) -> p t d", d=D), rows, ALU.add)\
                        .then_inc(added, 1)
                    if last_pair:
                        dve.wait_ge(added, chunk + 2)
                        for k in range(2):
                            last = take_stats(2 * c + k)
                        last.then_inc(stats_taken, 1)

                for w in range(AHEAD):
                    mask_unit(0, w)
                copy_v(0)

                def pair_body(pair, last_pair):
                    def chunk_body(c, parity, first, last_chunk):
                        chunk = NCH * pair + c
                        dve.wait_ge(pv_done, chunk + 1)
                        for w in range(UPC):
                            g = UPC * chunk + w
                            ahead = not last_chunk or w < UPC - AHEAD
                            u2, w2 = UPC * c + w + AHEAD, (w + AHEAD) % UPC
                            if w == 0 and not first:
                                spread_rden(chunk - 1, 1 - parity)
                            if ahead and w2 % 2 == 0:
                                admit_diagonal(pair, 2 * c + (w + AHEAD) // 2, w2 // 2)
                            for k in range(2):
                                if ahead:
                                    mask_half(pair, u2, w2, k)
                                if ahead and k == 1:
                                    finish_mask(pair, u2, w2, 2 * c + (w + AHEAD) // 2)
                                if k == VECTOR_GROUP // 2:
                                    copy_group(g, w, parity, VECTOR_GROUP)
                                if not ahead and not last_pair:
                                    lo_parts(dve, pair + 1, w - (UPC - AHEAD), k)
                                if w == 3 and k == 0 and not first:
                                    normalise_out(chunk - 1)
                            if w == 3 and not first:
                                add_out(chunk - 1, c - 1, last_pair)
                        if first:
                            dve.wait_ge(staged_out, 16 * STAGED)

                    each_chunk(dve, chunk_body)
                    final = NCH * pair + NCH - 1
                    spread_rden(final, 1)
                    if last_pair:
                        dve.wait_ge(stats_taken, NCH - 1)
                        norm_factors(dve, chained(dve, norm_steps), FIRST, squared_ready, root_ready, 1)
                    normalise_out(final)
                    if not last_pair:
                        for w in range(AHEAD):
                            mask_unit(pair + 1, w)
                    add_out(final, NCH - 1, last_pair)
                    if not last_pair:
                        copy_v(pair + 1)

                each_pair(dve, pair_body)
                dve.wait_ge(stats_taken, NCH)
    layer0.close()

    late = ExitStack()
    sb, _, _ = allocators(late)
    h = sb("h", [P, NT, D], F32)
    d_root = sb("d_root", [P, NT], F32)
    row_scale = sb("row_scale", [P, NT], F32)

    def split_rows(dve, t, h_ready, h_parts, parts_ready):
        dve.wait_ge(h_ready, t + 2)
        hi, lo = (h_parts[:, t:t + 2, k, :] for k in range(2))
        nc.vector.tensor_copy(hi, h[:, t:t + 2, :]).then_inc(parts_ready, 1)
        dve.wait_ge(parts_ready, t + 1)
        nc.vector.tensor_tensor(lo, h[:, t:t + 2, :], hi, ALU.subtract).then_inc(parts_ready, 1)

    def gather_early(pe, tiles, h_parts, parts_ready, banks, gathered):
        for j in range(NT):
            pe.wait_ge(parts_ready, 2 * (j // 2) + 2)
            for t in range(tiles):
                last = nc.tensor.matmul(banks[:, t, :], adjt[:, t, j, :], h_parts[:, j].rearrange("p a d -> p (a d)"),
                                        start=(j == 0), stop=(j == NT - 1))
                if j == NT - 1:
                    last.then_inc(gathered, 1)

    def fetch_tile(eng, t, slot, done):
        eng.dma_start(slot.rearrange("p j q -> p (j q)").bitcast(U16),
                      adjt[:, bass.ds(t, 1)].rearrange("p t j q -> p (t j q)").bitcast(U16)).then_inc(done, 16)

    def gather(slot, h_parts, ps_g, js):
        for j in js:
            last = nc.tensor.matmul(ps_g, slot[:, j, :], h_parts[:, j].rearrange("p a d -> p (a d)"),
                                    start=(j == 0), stop=(j == NT - 1))
        return last

    with ExitStack() as ctx:
        sb, ps, sem = allocators(ctx)
        EARLY = 6
        inv_norm = sb("inv_norm", [P, NT], F32)
        inc_scale = sb("inc_scale", [P, NT], F32)
        h_parts = sb("h_parts1", [P, NT, 2, D], F16)
        slots = sb("slots1", [P, 2, NT, P], F8)
        ps_g = ps("ps_g1", [P, EARLY + 2, 2 * D])
        fetched = [sem(f"fetched1{k}") for k in range(2)]
        steps, squared_ready, root_ready, stats_ready = (sem(f"{s}_1") for s in ("steps", "sq", "root", "stats"))
        h_ready, parts_ready = sem("h_ready1"), sem("parts_ready1")
        gathered = sem("gathered1")
        half_added = sem("half_added1")
        added = sem("added1")
        late_taken = sem("late_taken1")
        stats_taken = sem("stats_taken1")

        with nc.Block() as block:
            @block.sync
            def _(sp):
                for k in range(2):
                    fetch_tile(sp, EARLY + k, slots[:, k], fetched[k])
                with sp.Fori(EARLY // 2 + 1, NT // 2) as i:
                    for k in range(2):
                        sp.wait_ge(gathered, 2 * i + k - 1)
                        fetch_tile(sp, 2 * i + k, slots[:, k], fetched[k])

            @block.scalar
            def _(act):
                normalise(act, squared_ready, root_ready, stats_ready, h, h_ready, LAST)
                act.wait_ge(squared_ready, 2)
                nc.scalar.activation(root[:], deg[:], ACT.Sqrt).then_inc(root_ready, 1)
                take_root(act, ALL, squared_ready, root_ready, 3)
                take_root(act, FIRST, squared_ready, root_ready, 4)

            @block.tensor
            def _(pe):
                gather_early(pe, EARLY, h_parts, parts_ready, ps_g, gathered)
                with pe.Fori(0, (NT - EARLY) // 2) as i:
                    for k in range(2):
                        pe.wait_ge(fetched[k], 16 * i + 16)
                        pe.wait_ge(late_taken, 2 * i + k + 1)
                        stand_alone(pe)
                        gather(slots[:, k], h_parts, ps_g[:, EARLY + k, :], range(NT)).then_inc(gathered, 1)

            @block.vector
            def _(dve):
                dve.sem_inc(late_taken, 2)
                link = chained(dve, steps)
                split_rows(dve, 0, h_ready, h_parts, parts_ready)
                norm_factors(dve, link, LAST, squared_ready, root_ready, 1)
                dve.sem_inc(stats_ready, 1)
                for t in range(2, NT, 2):
                    split_rows(dve, t, h_ready, h_parts, parts_ready)
                dve.sem_inc(squared_ready, 1)
                dve.wait_ge(root_ready, 2)
                link(nc.vector.tensor_scalar(tmp[:], root[:], NORM_EPS, None, ALU.max))
                link(nc.vector.reciprocal(inv_norm[:], tmp[:]))
                link(nc.vector.tensor_scalar(inc_scale[:], inv_norm[:], 1.0, None, ALU.add))
                link(nc.vector.tensor_tensor(tmp[:], inc_scale[:], deg[:], ALU.mult))
                link(nc.vector.reciprocal(row_scale[:], tmp[:]))
                link(nc.vector.tensor_tensor(row_scale[:], row_scale[:], inc_scale[:], ALU.mult))
                link(nc.vector.tensor_scalar(squared[:], deg[:], 1.0, None, ALU.add))
                inverse_root(dve, link, ALL, d_root, squared_ready, root_ready, 3)

                def add_tile(t, bank):
                    rows = acc[:, bass.ds(t, 1), :].rearrange("p t d -> p (t d)")
                    scale = row_scale[:, bass.ds(t, 1)]
                    dve.wait_ge(gathered, t + 1)
                    nc.vector.scalar_tensor_tensor(out=rows, in0=ps_g[:, bank, 0:D], scalar=scale,
                                                   in1=rows, op0=ALU.mult, op1=ALU.add)\
                        .then_inc(half_added, 1)
                    dve.wait_ge(half_added, t + 1)
                    done = nc.vector.scalar_tensor_tensor(out=rows, in0=ps_g[:, bank, D:2 * D], scalar=scale,
                                                          in1=rows, op0=ALU.mult, op1=ALU.add)
                    done.then_inc(added, 1)
                    dve.wait_ge(added, t + 1)
                    if bank >= EARLY:
                        dve.sem_inc(late_taken, 1)
                    take_stats(t).then_inc(stats_taken, 1)

                for t in range(EARLY):
                    add_tile(t, t)
                with dve.Fori(EARLY // 2, NT // 2 - 1) as i:
                    for k in range(2):
                        add_tile(2 * i + k, EARLY + k)
                dve.wait_ge(stats_taken, FIRST.stop)
                norm_factors(dve, link, FIRST, squared_ready, root_ready, 4)
                for k in range(2):
                    add_tile(NT - 2 + k, EARLY + k)
                dve.wait_ge(stats_taken, NT)

    with ExitStack() as ctx:
        sb, ps, sem = allocators(ctx)
        PARTS = ((0, 0), (0, 1), (1, 0))
        hT = sb("hT2", [P, DC, N], F32)
        e_parts = sb("e_parts", [P, 2, DC, N], F16)
        support = sb("support", [P, NT, 2, D], F16)
        weight_sb = sb("weight_sb", [P, DC, D], F32)
        edge_sb = sb("edge_sb", [P, DC, D], F32)
        bias_rows = sb("bias_rows", [P, D], F32)
        node_rows = sb("node_rows", [P, D], F32)
        logits = sb("logits", [P, NT], F32)
        node_max = sb("node_max", [P, 3], F32)
        node_sum = sb("node_sum", [P, 3], F32)
        node_att = sb("node_att", [P, NT], F32)
        has_edge = sb("has_edge", [P, NT], F32)
        mask = sb("mask2", [P, 2, N], BF16)
        probs = sb("probs2", [P, 2, N], F32)
        probs_t = sb("probs_t2", [P, 2, 2, NT, P], F16)
        products = sb("products", [P, NT // 2, D], F32)
        row_max = sb("row_max2", [P, 2, 2], F32)
        neg_max = sb("neg_max2", [P, 2], F32)
        den = sb("den2", [P, 2], F32)
        rden = sb("rden2", [P, 2], F32)
        ps_s = ps("ps_s2", [P, 2, HALF])
        ps_t = ps("ps_t2", [P, HALF])
        ps_o = ps("ps_o2", [P, 2, 2 * D])
        ps_rows = ps_o[:].rearrange("p b (c q) -> p b c q", c=DC)

        w_in = sem("w_in2")
        steps, squared_ready, root_ready, stats_ready = (sem(f"{s}_2") for s in ("steps", "sq", "root", "stats"))
        h_ready, turned, evacuated = (sem(f"{s}_2") for s in ("h_ready", "turned", "evacuated"))
        max_ready, all_max, neg_ready = sem("max_ready"), sem("all_max"), sem("neg_ready")
        node_exp, all_sum = sem("node_exp"), sem("all_sum")
        mask_in = [sem(f"mask_in2{k}") for k in range(2)]
        half_full = sem("half_full2")
        half_free = sem("half_free2")
        hi_ready = sem("hi_ready2")
        masked = sem("masked2")
        exped = sem("exped2")
        t_full = sem("t_full2")
        t_hi = sem("t_hi2")
        t_free = sem("t_free2")
        pv_done = sem("pv_done2")
        scale_steps = sem("scale_steps2")
        half_added = sem("half_added2")
        added = sem("added2")
        stats_taken = sem("stats_taken2")

        E_HALF, SUPPORT_HALF = 0, 6

        def half_of(t, half):
            return 4 + half if isinstance(t, int) and t == 0 else 8 + 2 * t + half

        def each_round(eng, body):
            body(0, 0, True, True)
            with eng.Fori(0, NT // 2 - 1) as i:
                body(2 * i + 1, 1, False, True)
                body(2 * i + 2, 0, False, True)
            body(NT - 1, 1, False, False)

        with nc.Block() as block:
            @block.sync
            def _(sp):
                sp.dma_start(edge_sb[:], edge_w.rearrange("(c p) o -> p c o", p=P)).then_inc(w_in, 16)
                sp.dma_start(weight_sb[:], weight.rearrange("(c p) o -> p c o", p=P)).then_inc(w_in, 16)
                sp.dma_start(node_rows[:], node_w.rearrange("d a -> (d a)").partition_broadcast(P))\
                    .then_inc(w_in, 16)
                sp.dma_start(bias_rows[:], bias.partition_broadcast(P)).then_inc(w_in, 16)
                with sp.Fori(0, NT // 2) as i2:
                    for k in range(2):
                        sp.wait_ge(masked, 2 * i2 + k + 1)
                        sp.dma_start(mask[:, k, :], mask_dram[2 * i2 + k]).then_inc(mask_in[k], 16)

            @block.gpsimd
            def _(pool):
                pool.wait_ge(max_ready, 1)
                nc.gpsimd.partition_all_reduce(node_max[:, 1:2], node_max[:, 0:1], P, RMAX).then_inc(all_max, 1)
                pool.wait_ge(node_exp, 1)
                nc.gpsimd.partition_all_reduce(node_sum[:, 1:2], node_sum[:, 0:1], P, RADD).then_inc(all_sum, 1)

            @block.tensor
            def _(pe):
                pe.sem_inc(t_full, 4)
                pe.sem_inc(pv_done, 2)
                turn_rows(pe, h, h_ready, ps_rows, turned, evacuated)
                pe.wait_ge(w_in, 4 * 16)
                for n in range(4):
                    half, oc = n // 2, n % 2
                    pe.wait_ge(evacuated, (half + 1) * NT // 4)
                    pe.wait_ge(half_free, E_HALF + n + 1)
                    for c in range(2):
                        first = half * HALF + c * 512
                        for dc in range(DC):
                            last = nc.tensor.matmul(ps_s[:, n % 2, c * 512:(c + 1) * 512],
                                                    edge_sb[:, dc, oc * P:(oc + 1) * P],
                                                    hT[:, dc, first:first + 512],
                                                    start=(dc == 0), stop=(dc == DC - 1))
                    last.then_inc(half_full, 1)

                def scores(t, half):
                    pe.wait_ge(half_free, half_of(t, half) + 1)
                    for c in range(2):
                        first = half * HALF + c * 512
                        for dc in range(DC):
                            for a, b in PARTS:
                                last = nc.tensor.matmul(ps_s[:, half, c * 512:(c + 1) * 512],
                                                        e_parts[:, a, dc, bass.ds(t * P, P)],
                                                        e_parts[:, b, dc, first:first + 512],
                                                        start=(dc == 0 and (a, b) == PARTS[0]),
                                                        stop=(dc == DC - 1 and (a, b) == PARTS[-1]))
                    last.then_inc(half_full, 1)

                for half in range(2):
                    pe.wait_ge(half_free, 2 + 2 * (half + 1))
                    scores(0, half)
                for n in range(4):
                    pe.wait_ge(half_free, SUPPORT_HALF + n + 1)
                    for t in range(4):
                        first = (4 * n + t) * P
                        for dc in range(DC):
                            last = nc.tensor.matmul(ps_s[:, n % 2, t * D:(t + 1) * D],
                                                    hT[:, dc, first:first + P], weight_sb[:, dc, :],
                                                    start=(dc == 0), stop=(dc == DC - 1))
                    last.then_inc(half_full, 1)

                def turn(t, k, half):
                    pe.wait_ge(t_free, 2 * t + half + 1)
                    for n in range(NT // 2):
                        j = half * NT // 2 + n
                        last = nc.tensor.transpose(ps_t[:, n * P:(n + 1) * P], probs[:, k, j * P:(j + 1) * P],
                                                   ident[:])
                    last.then_inc(t_full, 1)

                def attend(t, k, half):
                    if half == 0:
                        pe.wait_ge(added, t + 1)
                        pe.wait_ge(t_free, 2 * t + 3)
                    for j in range(half * NT // 2, (half + 1) * NT // 2):
                        nc.tensor.matmul(ps_o[:, k, :], probs_t[:, k, 0, j, :],
                                         support[:, j].rearrange("p a d -> p (a d)"),
                                         start=(j == 0), stop=(j == NT - 1), skip_group_check=True)
                        last = nc.tensor.matmul(ps_o[:, k, 0:D], probs_t[:, k, 1, j, :], support[:, j, 0, :],
                                                start=False, stop=(j == NT - 1), skip_group_check=True)
                    if half == 1:
                        last.then_inc(pv_done, 1)

                def round_body(t, k, first, more):
                    for half in range(2):
                        if more:
                            scores(t + 1, half)
                        if half == 0:
                            pe.wait_ge(exped, t + 1)
                        turn(t, k, half)
                        if not first:
                            attend(t - 1, 1 - k, half)

                each_round(pe, round_body)
                for half in range(2):
                    attend(NT - 1, 1, half)

            @block.scalar
            def _(act):
                act.sem_inc(half_free, 2)
                normalise(act, squared_ready, root_ready, stats_ready, h, h_ready, LAST)
                for n in range(4):
                    half, oc = n // 2, n % 2
                    act.wait_ge(half_full, E_HALF + n + 1)
                    nc.scalar.activation(e_parts[:, 0, oc, half * HALF:(half + 1) * HALF], ps_s[:, n % 2, :],
                                         ACT.Copy).then_inc(hi_ready, 1)

                def exponentials(t, k):
                    act.wait_ge(masked, t + 3)
                    nc.scalar.activation(probs[:, k, :], probs[:, k, :], ACT.Exp, bias=neg_max[:, k:k + 1],
                                         accum_out=den[:, k:k + 1]).then_inc(exped, 1)

                exponentials(0, 0)
                for n in range(4):
                    act.wait_ge(half_full, SUPPORT_HALF + n + 1)
                    nc.scalar.activation(support[:, 4 * n:4 * n + 4, 0, :],
                                         ps_s[:, n % 2, :].rearrange("p (t d) -> p t d", d=D), ACT.Copy)\
                        .then_inc(hi_ready, 1)
                act.wait_ge(neg_ready, 1)
                nc.scalar.activation(node_att[:], logits[:], ACT.Exp, bias=node_max[:, 2:3],
                                     accum_out=node_sum[:, 0:1]).then_inc(node_exp, 1)

                def round_body(t, k, first, more):
                    act.wait_ge(pv_done, t + 1)
                    for half in range(2):
                        act.wait_ge(t_full, 2 * t + half + 5)
                        nc.scalar.activation(probs_t[:, k, 0, half * NT // 2:(half + 1) * NT // 2, :],
                                             ps_t[:].rearrange("p (j q) -> p j q", q=P), ACT.Copy)\
                            .then_inc(t_hi, 1)
                    if more:
                        exponentials(t + 1, 1 - k)

                each_round(act, round_body)
                take_root(act, FIRST, squared_ready, root_ready, 2)

            @block.vector
            def _(dve):
                dve.sem_inc(masked, 2)
                dve.sem_inc(t_free, 1)
                dve.sem_inc(added, 2)
                link = chained(dve, steps)
                norm_factors(dve, link, LAST, squared_ready, root_ready, 1)
                dve.sem_inc(stats_ready, 1)
                store_turned(dve, hT, ps_rows, turned, evacuated)

                def lo_of_half(n, full, hi, lo):
                    dve.wait_ge(hi_ready, n + 1)
                    nc.vector.tensor_tensor(lo, full, hi, ALU.subtract).then_inc(half_free, 1)

                dve.wait_ge(w_in, 4 * 16)
                dve.wait_ge(h_ready, NT)
                for n in range(4):
                    cols = slice(n // 2 * HALF, (n // 2 + 1) * HALF)
                    lo_of_half(n, ps_s[:, n % 2, :], e_parts[:, 0, n % 2, cols], e_parts[:, 1, n % 2, cols])
                    if n < 3:
                        rows = acc[:, (0, 6, 11)[n]:(6, 11, NT)[n], :]
                        link(nc.vector.tensor_tensor(
                            rows, rows, bias_rows[:].unsqueeze(1).to_broadcast([P, rows.shape[1], D]), ALU.add))

                def mask_half(t, k, half):
                    if half == 0:
                        dve.wait_ge(mask_in[k], 8 * t - 8 * k + 16)
                        dve.wait_ge(t_full, 2 * t + 2)
                    dve.wait_ge(half_full, half_of(t, half) + 1)
                    stand_alone(dve)
                    nc.vector.tensor_tensor_reduce(
                        probs[:, k, half * HALF:(half + 1) * HALF], ps_s[:, half, :],
                        mask[:, k, half * HALF:(half + 1) * HALF], 1.0, LOWEST, ALU.add, ALU.max,
                        row_max[:, k, half:half + 1]).then_inc(half_free, 1)

                def finish_mask(t, k):
                    dve.wait_ge(half_free, half_of(t, 1) + 3)
                    nc.vector.tensor_reduce(neg_max[:, k:k + 1], row_max[:, k, :], AX_X, ALU.max, negate=True)\
                        .then_inc(masked, 1)

                for half in range(2):
                    mask_half(0, 0, half)
                finish_mask(0, 0)

                def logits_of(tiles):
                    for t in tiles:
                        last = nc.vector.tensor_tensor_reduce(products[:, t % (NT // 2), :], h[:, t, :],
                                                              node_rows[:], 1.0, 0.0, ALU.mult, ALU.add,
                                                              logits[:, t:t + 1])
                    link(last)

                def support_lo(n):
                    tiles = slice(4 * n, 4 * n + 4)
                    lo_of_half(4 + n, ps_s[:, n % 2, :].rearrange("p (t d) -> p t d", d=D),
                               support[:, tiles, 0, :], support[:, tiles, 1, :])

                logits_of(range(NT // 2))
                support_lo(0)
                logits_of(range(NT // 2, NT))
                support_lo(1)
                nc.vector.tensor_reduce(node_max[:, 0:1], logits[:], AX_X, ALU.max).then_inc(max_ready, 1)
                support_lo(2)
                dve.wait_ge(all_max, 1)
                nc.vector.tensor_scalar(node_max[:, 2:3], node_max[:, 1:2], -1.0, None, ALU.mult)\
                    .then_inc(neg_ready, 1)
                support_lo(3)
                link(nc.vector.tensor_scalar(has_edge[:], deg[:], 1.0, None, ALU.min))

                def round_body(t, k, first, more):
                    dve.wait_ge(pv_done, t + 1)
                    for half in range(2):
                        if more:
                            mask_half(t + 1, 1 - k, half)
                        if more and half == 1:
                            finish_mask(t + 1, 1 - k)
                        dve.wait_ge(t_hi, 2 * t + half + 1)
                        tiles = slice(half * NT // 2, (half + 1) * NT // 2)
                        nc.vector.tensor_tensor(probs_t[:, k, 1, tiles, :],
                                                ps_t[:].rearrange("p (j q) -> p j q", q=P),
                                                probs_t[:, k, 0, tiles, :], ALU.subtract).then_inc(t_free, 1)
                    if first:
                        dve.wait_ge(all_sum, 1)
                        link(nc.vector.reciprocal(node_sum[:, 2:3], node_sum[:, 1:2]))
                        link(nc.vector.scalar_tensor_tensor(out=node_att[:], in0=node_att[:],
                                                            scalar=node_sum[:, 2:3], in1=has_edge[:],
                                                            op0=ALU.mult, op1=ALU.mult))
                    nc.vector.reciprocal(rden[:, k:k + 1], den[:, k:k + 1]).then_inc(scale_steps, 1)
                    dve.wait_ge(scale_steps, 2 * t + 1)
                    nc.vector.tensor_tensor(row_scale[:, bass.ds(t, 1)], rden[:, k:k + 1],
                                            node_att[:, bass.ds(t, 1)], ALU.mult).then_inc(scale_steps, 1)
                    if not first:
                        add_tile(t - 1, 1 - k)

                def add_tile(t, k):
                    dve.wait_ge(scale_steps, 2 * t + 2)
                    dve.wait_ge(pv_done, t + 3)
                    rows = acc[:, bass.ds(t, 1), :].rearrange("p t d -> p (t d)")
                    scale = row_scale[:, bass.ds(t, 1)]
                    nc.vector.scalar_tensor_tensor(out=rows, in0=ps_o[:, k, 0:D], scalar=scale, in1=rows,
                                                   op0=ALU.mult, op1=ALU.add).then_inc(half_added, 1)
                    dve.wait_ge(half_added, t + 1)
                    nc.vector.scalar_tensor_tensor(out=rows, in0=ps_o[:, k, D:2 * D], scalar=scale, in1=rows,
                                                   op0=ALU.mult, op1=ALU.add).then_inc(added, 1)
                    dve.wait_ge(added, t + 3)
                    take_stats(t).then_inc(stats_taken, 1)

                each_round(dve, round_body)
                dve.wait_ge(stats_taken, NT - 1)
                norm_factors(dve, link, FIRST, squared_ready, root_ready, 2, scale=d_root)
                add_tile(NT - 1, 1)
                dve.wait_ge(stats_taken, NT)

    with ExitStack() as ctx:
        sb, ps, sem = allocators(ctx)
        AHEAD3 = 3
        w3_sb = sb("w3_sb", [P, DC, D], F32)
        w3_t = sb("w3_t", [P, DC, D], F32)
        b3_rows = sb("b3_rows", [P, D], F32)
        with_self = sb("with_self", [P, 2, D], F32)
        z = sb("z", [P, 2, D], F32)
        z_t = sb("z_t", [P, 2, DC, P], F32)
        linear = sb("linear", [P, 2, D], F32)
        h_parts = sb("h_parts3", [P, NT, 2, D], F16)
        slots = sb("slots3", [P, 2, NT, P], F8)
        ps_g = ps("ps_g3", [P, AHEAD3 + 1, 2 * D])
        ps_z = ps("ps_z", [P, 2, 512])
        ps_f = ps("ps_f", [P, 2, 512])

        fetched = [sem(f"fetched3{k}") for k in range(2)]
        w_in = sem("w_in3")
        steps, squared_ready, root_ready, stats_ready = (sem(f"{s}_3") for s in ("steps", "sq", "root", "stats"))
        h_ready, parts_ready = sem("h_ready3"), sem("parts_ready3")
        w3_turned, w3_ready = sem("w3_turned"), sem("w3_ready")
        gathered, z_steps, z_ready = sem("gathered3"), sem("z_steps"), sem("z_ready")
        z_turned, z_t_ready = sem("z_turned"), sem("z_t_ready")
        final_ready, linear_ready, rows_ready = sem("final_ready"), sem("linear_ready"), sem("rows_ready")
        stored = sem("stored")

        def each_round(eng, body):
            with eng.Fori(0, (NT - AHEAD3) // 4) as i:
                for n in range(4):
                    body(4 * i + n, n, True)
            for t in range((NT - AHEAD3) // 4 * 4, NT):
                body(t, t % 4, t < NT - AHEAD3)

        with nc.Block() as block:
            @block.sync
            def _(sp):
                sp.dma_start(w3_sb[:], W3.rearrange("(c p) i -> p c i", p=P)).then_inc(w_in, 16)
                sp.dma_start(b3_rows[:], b3.partition_broadcast(P)).then_inc(w_in, 16)
                with sp.Fori(0, NT) as t:
                    sp.wait_ge(rows_ready, t + 1)
                    sp.dma_start(out[bass.ds(t * P, P), :],
                                 acc[:, bass.ds(t, 1), :].rearrange("p t d -> p (t d)")).then_inc(stored, 16)
                sp.wait_ge(stored, 16 * NT)

            @block.gpsimd
            def _(pool):
                for n in range(2):
                    fetch_tile(pool, AHEAD3 + n, slots[:, n], fetched[n])
                fetch = (NT - AHEAD3) // 2
                with pool.Fori(1, fetch) as i:
                    for n in range(2):
                        pool.wait_ge(gathered, AHEAD3 + 2 * i + n - 1)
                        stand_alone(pool)
                        fetch_tile(pool, AHEAD3 + 2 * i + n, slots[:, n], fetched[n])
                pool.wait_ge(gathered, NT - 2)
                fetch_tile(pool, NT - 1, slots[:, 0], fetched[0])

            @block.tensor
            def _(pe):
                pe.wait_ge(w_in, 2 * 16)
                for ic in range(DC):
                    for oc in range(DC):
                        last = nc.tensor.transpose(ps_z[:, ic, oc * P:(oc + 1) * P],
                                                   w3_sb[:, oc, ic * P:(ic + 1) * P], ident[:])
                last.then_inc(w3_turned, 1)
                gather_early(pe, AHEAD3, h_parts, parts_ready, ps_g, gathered)
                pe.wait_ge(w3_ready, 1)

                def round_body(t, n, more):
                    k, bank, slot = n % 2, (n + AHEAD3) % 4, n % 2
                    if more:
                        pe.wait_ge(fetched[slot], 8 * (t - k) + 16)
                        stand_alone(pe)
                        gather(slots[:, slot], h_parts, ps_g[:, bank, :], range(NT // 2))
                    pe.wait_ge(z_ready, t + 1)
                    for dc in range(DC):
                        last = nc.tensor.transpose(ps_z[:, k, dc * P:(dc + 1) * P],
                                                   z[:, k, dc * P:(dc + 1) * P], ident[:])
                    last.then_inc(z_turned, 1)
                    if more:
                        gather(slots[:, slot], h_parts, ps_g[:, bank, :], range(NT // 2, NT))\
                            .then_inc(gathered, 1)
                    pe.wait_ge(z_t_ready, t + 1)
                    for dc in range(DC):
                        last = nc.tensor.matmul(ps_f[:, k, 0:D], z_t[:, k, dc, :], w3_t[:, dc, :],
                                                start=(dc == 0), stop=(dc == DC - 1))
                    last.then_inc(final_ready, 1)

                each_round(pe, round_body)

            @block.scalar
            def _(act):
                normalise(act, squared_ready, root_ready, stats_ready, h, h_ready, LAST)
                act.wait_ge(w3_turned, 1)
                nc.scalar.activation(w3_t[:], ps_z[:, :, 0:D], ACT.Copy).then_inc(w3_ready, 1)

                def round_body(t, n, more):
                    k = n % 2
                    act.wait_ge(z_turned, t + 1)
                    nc.scalar.activation(z_t[:, k], ps_z[:, k, 0:D].rearrange("p (c q) -> p c q", c=DC), ACT.Copy)\
                        .then_inc(z_t_ready, 1)

                each_round(act, round_body)

            @block.vector
            def _(dve):
                link = chained(dve, steps)
                split_rows(dve, 0, h_ready, h_parts, parts_ready)
                norm_factors(dve, link, LAST, squared_ready, root_ready, 1, scale=d_root)
                dve.sem_inc(stats_ready, 1)
                for t in range(2, NT, 2):
                    split_rows(dve, t, h_ready, h_parts, parts_ready)
                dve.wait_ge(w_in, 2 * 16)

                def add_up(t, n):
                    k = n % 2
                    dve.wait_ge(gathered, t + 1)
                    nc.vector.tensor_tensor(with_self[:, k, :], ps_g[:, n, 0:D],
                                            h[:, bass.ds(t, 1), :].rearrange("p t d -> p (t d)"), ALU.add)\
                        .then_inc(z_steps, 1)
                    dve.wait_ge(z_steps, t + 1)
                    nc.vector.tensor_tensor(z[:, k, :], ps_g[:, n, D:2 * D], with_self[:, k, :], ALU.add)\
                        .then_inc(z_ready, 1)

                def finish(t, n):
                    k = n % 2
                    dve.wait_ge(final_ready, t + 1)
                    rows = acc[:, bass.ds(t, 1), :].rearrange("p t d -> p (t d)")
                    nc.vector.scalar_tensor_tensor(out=linear[:, k, :], in0=ps_f[:, k, 0:D],
                                                   scalar=d_root[:, bass.ds(t, 1)], in1=b3_rows[:],
                                                   op0=ALU.mult, op1=ALU.add).then_inc(linear_ready, 1)
                    dve.wait_ge(linear_ready, t + 1)
                    nc.vector.scalar_tensor_tensor(out=rows, in0=linear[:, k, :], scalar=0.0, in1=rows,
                                                   op0=ALU.max, op1=ALU.add).then_inc(rows_ready, 1)

                add_up(0, 0)

                def round_body(t, n, more):
                    if more or t < NT - 1:
                        add_up(t + 1, (n + 1) % 4)
                    finish(t, n)

                each_round(dve, round_body)
    late.close()
    whole.close()


_INS = ['x', 'adj', 'L0_gnn_Wks', 'L0_gnn_Wqs', 'L0_gnn_Wvs', 'L0_gnn_Wo', 'L2_gnn_weight', 'L2_gnn_bias',
        'L2_gnn_node_w', 'L2_gnn_edge_w', 'L3_gnn_W', 'L3_gnn_b']


def kernel(**inputs):
    import numpy as _np
    import concourse.bacc as _bacc
    from concourse import mybir as _mybir
    from concourse.bass_utils import run_bass_kernel_spmd as _run

    nc = _bacc.Bacc("TRN2", target_bir_lowering=False, num_devices=1)
    arrays, args = {}, []
    for name in _INS:
        a = _np.ascontiguousarray(inputs[name])
        arrays[f"in_{name}_dram"] = a
        args.append(nc.dram_tensor(f"in_{name}_dram", a.shape, _mybir.dt.from_np(a.dtype), kind="ExternalInput").ap())
    args.append(nc.dram_tensor("out_dram", (N, D), F32, kind="ExternalOutput").ap())
    program(nc, *args)
    r = _run(nc, [arrays], core_ids=[0])
    return r.results[0]["out_dram"]
```
